# Optimizing a Trainium2 kernel written in Bass

```python
import numpy as np
import jax
import jax.numpy as jnp

def _softmax(x, axis=-1):
    return jax.nn.softmax(x, axis=axis)

def _gelu(x):
    return jax.nn.gelu(x, approximate=True)

def _silu(x):
    return jax.nn.silu(x)

def _sigmoid(x):
    return jax.nn.sigmoid(x)

def _layernorm(x, axis=-1, eps=1e-05):
    m = jnp.mean(x, axis=axis, keepdims=True)
    v = jnp.var(x, axis=axis, keepdims=True)
    return (x - m) / jnp.sqrt(v + eps)

def _scatter_add(tgt, idx, src, axis=0):
    return tgt.at[idx].add(src)

def _segment_sum(src, seg, n):
    return jax.ops.segment_sum(src, seg, n)
kernel_name = 'mk_seq_preln_d2_jaxref_r8_48e5ea'

def setup_inputs(seed: int=0):
    np.random.seed(seed)
    _w = jnp.asarray

    def _L0_attn_setup():
        import jax, jax.numpy as jnp
        import numpy as np
        DIMS = 256
        HEAD = 16
        HD = DIMS // HEAD
        HD2 = HD // 2
        B, C = (1, 256)

        def layernorm(x, g, b, eps=1e-05):
            mu = x.mean(-1, keepdims=True)
            var = x.var(-1, keepdims=True)
            return (x - mu) / jnp.sqrt(var + eps) * g + b

        def rotary_freqs():
            f = (8000.0 / 200.0) ** jnp.linspace(0.0, 1.0, HD2) * 200.0 / 1000.0
            return 200.0 * f / 1000.0

        def apply_rotary(y, xa):
            t = jnp.arange(y.shape[2], dtype=jnp.float32)
            ang = jnp.einsum('i,j->ij', t, rotary_freqs())
            m = jnp.linalg.norm(xa, axis=-1)
            rr = (m[..., None] * jnp.cos(ang))[:, None]
            ri = (m[..., None] * jnp.sin(ang))[:, None]
            yp = y.reshape(*y.shape[:-1], HD2, 2)
            yr, yi = (yp[..., 0], yp[..., 1])
            out_r = yr * rr - yi * ri
            out_i = yr * ri + yi * rr
            return jnp.stack([out_r, out_i], axis=-1).reshape(y.shape)
        key = jax.random.key(seed)
        ks = jax.random.split(key, 4)
        s = 0.02
        return {'x': jax.random.normal(ks[0], (B, C, DIMS), jnp.float32), 'ln_q_g': jnp.ones((DIMS,), jnp.float32), 'ln_q_b': jnp.zeros((DIMS,), jnp.float32), 'Wq': jax.random.normal(ks[1], (DIMS, DIMS), jnp.float32) * s, 'bq': jnp.zeros((DIMS,), jnp.float32), 'ln_kv_g': jnp.ones((DIMS,), jnp.float32), 'ln_kv_b': jnp.zeros((DIMS,), jnp.float32), 'Wkv': jax.random.normal(ks[2], (DIMS, 2 * DIMS), jnp.float32) * s, 'bkv': jnp.zeros((2 * DIMS,), jnp.float32), 'ln_h_g': jnp.ones((HD,), jnp.float32), 'ln_h_b': jnp.zeros((HD,), jnp.float32), 'Wo': jax.random.normal(ks[3], (DIMS, DIMS), jnp.float32) * s, 'bo': jnp.zeros((DIMS,), jnp.float32)}
    _L0_attn_in = _L0_attn_setup()

    def _L0_ffn_setup():
        import jax, jax.numpy as jnp
        import numpy as np
        E, K, H, F_EXP = (64, 6, 256, 176)
        B, S = (1, 64)

        def _swiglu(x, g, v, o):
            return jax.nn.silu(x @ g) * (x @ v) @ o
        key = jax.random.key(seed)
        ks = jax.random.split(key, 8)
        s_h = 1.0 / np.sqrt(H)
        s_f = 1.0 / np.sqrt(F_EXP)
        return {'hidden_states': jax.random.normal(ks[0], (B, S, H), jnp.float32), 'w_router': jax.random.normal(ks[1], (E, H), jnp.float32) * s_h, 'wg': jax.random.normal(ks[2], (E, H, F_EXP), jnp.float32) * s_h, 'wv': jax.random.normal(ks[3], (E, H, F_EXP), jnp.float32) * s_h, 'wo': jax.random.normal(ks[4], (E, F_EXP, H), jnp.float32) * s_f, 'swg': jax.random.normal(ks[5], (H, F_EXP), jnp.float32) * s_h, 'swv': jax.random.normal(ks[6], (H, F_EXP), jnp.float32) * s_h, 'swo': jax.random.normal(ks[7], (F_EXP, H), jnp.float32) * s_f}
    _L0_ffn_in = _L0_ffn_setup()

    def _L1_attn_setup():
        import jax, jax.numpy as jnp
        import numpy as np
        B, S, E = (1, 256, 256)
        H = 16
        DN = 128
        DR = 64
        DV = 128
        R = 64
        QLR = 192
        EPS = 1e-06
        ROPE_BASE = 10000.0

        def _rmsnorm(x, w):
            var = jnp.mean(jnp.square(x), axis=-1, keepdims=True)
            return x * jax.lax.rsqrt(var + EPS) * w

        def _rope_cos_sin(seqlen):
            inv_freq = 1.0 / ROPE_BASE ** (jnp.arange(0, DR, 2, dtype=jnp.float32) / DR)
            ang = jnp.arange(seqlen, dtype=jnp.float32)[:, None] * inv_freq[None, :]
            cos = jnp.concatenate([jnp.cos(ang), jnp.cos(ang)], axis=-1)
            sin = jnp.concatenate([jnp.sin(ang), jnp.sin(ang)], axis=-1)
            return (cos, sin)

        def _rotate_half(x):
            x1, x2 = jnp.split(x, 2, axis=-1)
            return jnp.concatenate([-x2, x1], axis=-1)
        key = jax.random.key(seed)
        ks = jax.random.split(key, 8)
        sd = lambda fan_in: 1.0 / np.sqrt(fan_in)
        return {'x': jax.random.normal(ks[0], (B, S, E), jnp.float32), 'w_q_a': jax.random.normal(ks[1], (E, QLR), jnp.float32) * sd(E), 'q_a_ln_w': jnp.ones((QLR,), jnp.float32), 'w_q_b': jax.random.normal(ks[2], (QLR, H * (DN + DR)), jnp.float32) * sd(QLR), 'w_kv_a': jax.random.normal(ks[3], (E, R + DR), jnp.float32) * sd(E), 'kv_a_ln_w': jnp.ones((R,), jnp.float32), 'w_kv_b': jax.random.normal(ks[4], (R, H * (DN + DV)), jnp.float32) * sd(R), 'w_o': jax.random.normal(ks[5], (H * DV, E), jnp.float32) * sd(H * DV)}
    _L1_attn_in = _L1_attn_setup()

    def _L1_ffn_setup():
        import jax, jax.numpy as jnp
        import numpy as np
        B, S, D, H = (4, 256, 256, 1024)

        def fwht(x):
            orig_shape = x.shape
            n = orig_shape[-1]
            x = x.reshape(-1, n)
            h = 1
            while h < n:
                xb = x.reshape(-1, n // (2 * h), 2, h)
                a = xb[:, :, 0, :]
                b = xb[:, :, 1, :]
                x = jnp.stack([a + b, a - b], axis=2).reshape(-1, n)
                h *= 2
            scale = jnp.asarray(1.0 / np.sqrt(n), dtype=x.dtype)
            return (x * scale).reshape(orig_shape)
        key = jax.random.key(seed)
        kx, k1, k2, k3 = jax.random.split(key, 4)
        x = jax.random.normal(kx, (B, S, D), dtype=jnp.float32)
        W1 = jax.random.normal(k1, (H, D), dtype=jnp.float32) * (1.0 / np.sqrt(D))
        W2 = jax.random.normal(k2, (D, H), dtype=jnp.float32) * (1.0 / np.sqrt(H))
        W3 = jax.random.normal(k3, (H, D), dtype=jnp.float32) * (1.0 / np.sqrt(D))
        return {'x': x, 'W1': W1, 'W2': W2, 'W3': W3}
    _L1_ffn_in = _L1_ffn_setup()
    _d = {'L0_attn_x': _L0_attn_in['x'], 'L0_attn_ln_q_g': _L0_attn_in['ln_q_g'], 'L0_attn_ln_q_b': _L0_attn_in['ln_q_b'], 'L0_attn_Wq': _L0_attn_in['Wq'], 'L0_attn_bq': _L0_attn_in['bq'], 'L0_attn_ln_kv_g': _L0_attn_in['ln_kv_g'], 'L0_attn_ln_kv_b': _L0_attn_in['ln_kv_b'], 'L0_attn_Wkv': _L0_attn_in['Wkv'], 'L0_attn_bkv': _L0_attn_in['bkv'], 'L0_attn_ln_h_g': _L0_attn_in['ln_h_g'], 'L0_attn_ln_h_b': _L0_attn_in['ln_h_b'], 'L0_attn_Wo': _L0_attn_in['Wo'], 'L0_attn_bo': _L0_attn_in['bo'], 'L0_ffn_w_router': _L0_ffn_in['w_router'], 'L0_ffn_wg': _L0_ffn_in['wg'], 'L0_ffn_wv': _L0_ffn_in['wv'], 'L0_ffn_wo': _L0_ffn_in['wo'], 'L0_ffn_swg': _L0_ffn_in['swg'], 'L0_ffn_swv': _L0_ffn_in['swv'], 'L0_ffn_swo': _L0_ffn_in['swo'], 'L1_attn_w_q_a': _L1_attn_in['w_q_a'], 'L1_attn_q_a_ln_w': _L1_attn_in['q_a_ln_w'], 'L1_attn_w_q_b': _L1_attn_in['w_q_b'], 'L1_attn_w_kv_a': _L1_attn_in['w_kv_a'], 'L1_attn_kv_a_ln_w': _L1_attn_in['kv_a_ln_w'], 'L1_attn_w_kv_b': _L1_attn_in['w_kv_b'], 'L1_attn_w_o': _L1_attn_in['w_o'], 'L1_ffn_W1': _L1_ffn_in['W1'], 'L1_ffn_W2': _L1_ffn_in['W2'], 'L1_ffn_W3': _L1_ffn_in['W3']}
    _x0 = _d['L0_attn_x']
    _d['L0_attn_x'] = jax.random.normal(jax.random.fold_in(jax.random.key(seed), 1), (2, 1024, 256), dtype=_x0.dtype)
    del _x0
    return _d

def reference(L0_attn_x, L0_attn_ln_q_g, L0_attn_ln_q_b, L0_attn_Wq, L0_attn_bq, L0_attn_ln_kv_g, L0_attn_ln_kv_b, L0_attn_Wkv, L0_attn_bkv, L0_attn_ln_h_g, L0_attn_ln_h_b, L0_attn_Wo, L0_attn_bo, L0_ffn_w_router, L0_ffn_wg, L0_ffn_wv, L0_ffn_wo, L0_ffn_swg, L0_ffn_swv, L0_ffn_swo, L1_attn_w_q_a, L1_attn_q_a_ln_w, L1_attn_w_q_b, L1_attn_w_kv_a, L1_attn_kv_a_ln_w, L1_attn_w_kv_b, L1_attn_w_o, L1_ffn_W1, L1_ffn_W2, L1_ffn_W3):

    def _L0_attn_ref(x, ln_q_g, ln_q_b, Wq, bq, ln_kv_g, ln_kv_b, Wkv, bkv, ln_h_g, ln_h_b, Wo, bo):
        import jax, jax.numpy as jnp
        import numpy as np
        DIMS = 256
        HEAD = 16
        HD = DIMS // HEAD
        HD2 = HD // 2
        B, C = (1, 256)

        def layernorm(x, g, b, eps=1e-05):
            mu = x.mean(-1, keepdims=True)
            var = x.var(-1, keepdims=True)
            return (x - mu) / jnp.sqrt(var + eps) * g + b

        def rotary_freqs():
            f = (8000.0 / 200.0) ** jnp.linspace(0.0, 1.0, HD2) * 200.0 / 1000.0
            return 200.0 * f / 1000.0

        def apply_rotary(y, xa):
            t = jnp.arange(y.shape[2], dtype=jnp.float32)
            ang = jnp.einsum('i,j->ij', t, rotary_freqs())
            m = jnp.linalg.norm(xa, axis=-1)
            rr = (m[..., None] * jnp.cos(ang))[:, None]
            ri = (m[..., None] * jnp.sin(ang))[:, None]
            yp = y.reshape(*y.shape[:-1], HD2, 2)
            yr, yi = (yp[..., 0], yp[..., 1])
            out_r = yr * rr - yi * ri
            out_i = yr * ri + yi * rr
            return jnp.stack([out_r, out_i], axis=-1).reshape(y.shape)
        b, c, d = x.shape
        q = (layernorm(x, ln_q_g, ln_q_b) @ Wq + bq).reshape(b, c, HEAD, HD).transpose(0, 2, 1, 3)
        kv = (layernorm(x, ln_kv_g, ln_kv_b) @ Wkv + bkv).reshape(b, c, 2, HEAD, HD)
        k = kv[:, :, 0].transpose(0, 2, 1, 3)
        v = kv[:, :, 1].transpose(0, 2, 1, 3)
        scale = HD ** (-0.25)
        q = q * scale
        k = k * scale
        q = apply_rotary(q, x)
        k = apply_rotary(k, x)
        qn = layernorm(q, ln_h_g, ln_h_b)
        kn = layernorm(k, ln_h_g, ln_h_b)
        logits = jnp.einsum('bhqd,bhkd->bhqk', qn, kn) / jnp.sqrt(jnp.float32(HD))
        att = jax.nn.softmax(logits, axis=-1)
        a = jnp.einsum('bhqk,bhkd->bhqd', att, v)
        a = a.transpose(0, 2, 1, 3).reshape(b, c, d)
        return a @ Wo + bo

    def _L0_ffn_ref(hidden_states, w_router, wg, wv, wo, swg, swv, swo):
        import jax, jax.numpy as jnp
        import numpy as np
        E, K, H, F_EXP = (64, 6, 256, 176)
        B, S = (1, 64)

        def _swiglu(x, g, v, o):
            return jax.nn.silu(x @ g) * (x @ v) @ o
        b, s, h = hidden_states.shape
        x = hidden_states.reshape(-1, h)
        T = x.shape[0]
        scores = jax.nn.softmax(x @ w_router.T, axis=-1)
        topw, topi = jax.lax.top_k(scores, K)
        combine = jnp.zeros((T, E), x.dtype).at[jnp.arange(T)[:, None], topi].add(topw)

        def body(acc, ws):
            g, v, o, cw = ws
            return (acc + cw[:, None] * _swiglu(x, g, v, o), None)
        routed, _ = jax.lax.scan(body, jnp.zeros_like(x), (wg, wv, wo, combine.T))
        shared = _swiglu(x, swg, swv, swo)
        return (routed + shared).reshape(b, s, h)

    def _L1_attn_ref(x, w_q_a, q_a_ln_w, w_q_b, w_kv_a, kv_a_ln_w, w_kv_b, w_o):
        import jax, jax.numpy as jnp
        import numpy as np
        B, S, E = (1, 256, 256)
        H = 16
        DN = 128
        DR = 64
        DV = 128
        R = 64
        QLR = 192
        EPS = 1e-06
        ROPE_BASE = 10000.0

        def _rmsnorm(x, w):
            var = jnp.mean(jnp.square(x), axis=-1, keepdims=True)
            return x * jax.lax.rsqrt(var + EPS) * w

        def _rope_cos_sin(seqlen):
            inv_freq = 1.0 / ROPE_BASE ** (jnp.arange(0, DR, 2, dtype=jnp.float32) / DR)
            ang = jnp.arange(seqlen, dtype=jnp.float32)[:, None] * inv_freq[None, :]
            cos = jnp.concatenate([jnp.cos(ang), jnp.cos(ang)], axis=-1)
            sin = jnp.concatenate([jnp.sin(ang), jnp.sin(ang)], axis=-1)
            return (cos, sin)

        def _rotate_half(x):
            x1, x2 = jnp.split(x, 2, axis=-1)
            return jnp.concatenate([-x2, x1], axis=-1)
        b, s, _ = x.shape
        q_a = _rmsnorm(x @ w_q_a, q_a_ln_w)
        q = (q_a @ w_q_b).reshape(b, s, H, DN + DR)
        q_nope, q_pe = (q[..., :DN], q[..., DN:])
        ckv_kpe = x @ w_kv_a
        ckv = _rmsnorm(ckv_kpe[..., :R], kv_a_ln_w)
        k_pe = ckv_kpe[..., R:].reshape(b, s, 1, DR)
        cos, sin = _rope_cos_sin(s)
        cos, sin = (cos[None, :, None, :], sin[None, :, None, :])
        q_pe = q_pe * cos + _rotate_half(q_pe) * sin
        k_pe = k_pe * cos + _rotate_half(k_pe) * sin
        w_kv = w_kv_b.reshape(R, H, DN + DV)
        w_uk = w_kv[..., :DN]
        w_uv = w_kv[..., DN:]
        w_o3 = w_o.reshape(H, DV, E)
        w_o_abs = jnp.einsum('rhd,hde->hre', w_uv, w_o3)
        q_abs = jnp.einsum('bshd,rhd->bshr', q_nope, w_uk)
        q_full = jnp.concatenate([q_abs, q_pe], axis=-1)
        k_full = jnp.concatenate([ckv, k_pe[:, :, 0, :]], axis=-1)
        sm_scale = (DN + DR) ** (-0.5)
        scores = jnp.einsum('bqhd,bkd->bhqk', q_full, k_full) * sm_scale
        causal = jnp.tril(jnp.ones((s, s), dtype=bool))
        scores = jnp.where(causal[None, None], scores, jnp.finfo(scores.dtype).min)
        attn = jax.nn.softmax(scores, axis=-1)
        o_ckv = jnp.einsum('bhqk,bkr->bqhr', attn, ckv)
        y = jnp.einsum('bqhr,hre->bqe', o_ckv, w_o_abs)
        return y

    def _L1_ffn_ref(x, W1, W2, W3):
        import jax, jax.numpy as jnp
        import numpy as np
        B, S, D, H = (4, 256, 256, 1024)

        def fwht(x):
            orig_shape = x.shape
            n = orig_shape[-1]
            x = x.reshape(-1, n)
            h = 1
            while h < n:
                xb = x.reshape(-1, n // (2 * h), 2, h)
                a = xb[:, :, 0, :]
                b = xb[:, :, 1, :]
                x = jnp.stack([a + b, a - b], axis=2).reshape(-1, n)
                h *= 2
            scale = jnp.asarray(1.0 / np.sqrt(n), dtype=x.dtype)
            return (x * scale).reshape(orig_shape)
        up_gate = jnp.einsum('bsd,hd->bsh', x, W1)
        up_lin = jnp.einsum('bsd,hd->bsh', x, W3)
        hidden = jax.nn.silu(up_gate) * up_lin
        hidden = fwht(hidden)
        out = jnp.einsum('bsh,dh->bsd', hidden, W2)
        return out
    x = L0_attn_x
    x = x + _L0_attn_ref(_layernorm(x, axis=-1), L0_attn_ln_q_g, L0_attn_ln_q_b, L0_attn_Wq, L0_attn_bq, L0_attn_ln_kv_g, L0_attn_ln_kv_b, L0_attn_Wkv, L0_attn_bkv, L0_attn_ln_h_g, L0_attn_ln_h_b, L0_attn_Wo, L0_attn_bo)
    x = x + _L0_ffn_ref(_layernorm(x, axis=-1), L0_ffn_w_router, L0_ffn_wg, L0_ffn_wv, L0_ffn_wo, L0_ffn_swg, L0_ffn_swv, L0_ffn_swo)
    x = x + _L1_attn_ref(_layernorm(x, axis=-1), L1_attn_w_q_a, L1_attn_q_a_ln_w, L1_attn_w_q_b, L1_attn_w_kv_a, L1_attn_kv_a_ln_w, L1_attn_w_kv_b, L1_attn_w_o)
    x = x + _L1_ffn_ref(_layernorm(x, axis=-1), L1_ffn_W1, L1_ffn_W2, L1_ffn_W3)
    return x

_drawn_inputs = setup_inputs


def setup_inputs(seed=0):
    import zlib

    import numpy as np

    out = dict(_drawn_inputs(seed))
    spreads = {'L0_attn_ln_q_g': (1.0, 0.6),
     'L0_attn_ln_q_b': (0.0, 0.8),
     'L0_attn_bq': (0.0, 2.0),
     'L0_attn_ln_kv_g': (1.0, 0.6),
     'L0_attn_ln_kv_b': (0.0, 0.519),
     'L0_attn_bkv': (0.0, 0.1),
     'L0_attn_ln_h_g': (1.0, 0.6),
     'L0_attn_ln_h_b': (0.0, 2.0),
     'L0_attn_bo': (0.0, 0.1),
     'L1_attn_q_a_ln_w': (1.0, 0.2),
     'L1_attn_kv_a_ln_w': (1.0, 0.2)}
    factors = {'L0_attn_Wq': 8.0, 'L0_attn_Wkv': 3.023}
    for name, (base, spread) in spreads.items():
        noise = np.random.default_rng([zlib.crc32(name.encode()), seed]).standard_normal(out[name].shape)
        drawn = base * np.exp(spread * noise) if base else spread * noise
        out[name] = jnp.asarray(drawn.astype(out[name].dtype))
    for name, factor in factors.items():
        out[name] = (out[name] * factor).astype(out[name].dtype)
    return out
```

```python
from contextlib import ExitStack

import numpy as np

import concourse.bass as bass
from concourse import mybir

ALU = mybir.AluOpType
ACT = mybir.ActivationFunctionType
AX = mybir.AxisListType
F32 = mybir.dt.float32
BF16 = mybir.dt.bfloat16
F32R = mybir.dt.float32r
U32 = mybir.dt.uint32

P = 128
B, S, D = 2, 1024, 256
T = B * S // P
TB = S // P
DK = D // P
LN_EPS = 1e-5

H0, HD = 16, 16
NP = 6
QK0 = NP * HD
ROWS0 = QK0 + 3
NG = B * H0 // 4
VW = HD + 1
VG = 3 * VW + 32


def reuse(eng, used, t, depth, per=1):
    if not isinstance(t, int) or t >= depth:
        eng.wait_ge(used, (t - (depth - 1)) * per)


def tables():
    t = np.arange(S, dtype=np.float32)
    f = (np.float32(8000.0 / 200.0) ** np.linspace(0.0, 1.0, HD // 2, dtype=np.float32)) * np.float32(200.0)
    f = (np.float32(200.0) * (f / np.float32(1000.0)) / np.float32(1000.0)).astype(np.float32)
    ang = (t[:, None] * f[None, :]).astype(np.float32)
    c, s = np.cos(ang), np.sin(ang)
    own = np.repeat(c, 2, axis=1)
    other = np.stack([-s, s], axis=-1).reshape(S, HD)
    rot = np.stack([own, other], axis=1)
    rot = rot.reshape(TB, P, 2, HD).transpose(1, 0, 2, 3)
    inv = np.float32(1.0) / np.float32(10000.0) ** (np.arange(0, 64, 2, dtype=np.float32) / np.float32(64))
    ang = (t[:, None] * inv[None, :]).astype(np.float32)
    c, s = np.cos(ang), np.sin(ang)
    rope = np.stack([np.concatenate([c, c], 1), np.concatenate([-s, s], 1)], axis=1)
    rope = rope.reshape(TB, P, 2, 64).transpose(1, 0, 2, 3)
    i = np.arange(P)
    bits = np.zeros((P, P), np.int64)
    for n in range(7):
        bits += (i[:, None] >> n & 1) * (i[None, :] >> n & 1)
    hadamard = np.where(bits % 2, -1.0, 1.0) / 32.0
    return {n: np.ascontiguousarray(t, dtype=np.float32) for n, t in (
        ("rot_table", rot), ("rope_table", rope), ("hadamard_table", hadamard))}


class Mem:

    def __init__(self, nc, ctx, suffix=""):
        self.nc, self.ctx, self.suffix, self.sems = nc, ctx, suffix, []

    def sb(self, name, shape, dt=F32):
        return self.ctx.enter_context(self.nc.sbuf_tensor(name + self.suffix, shape, dt))

    def ps(self, name, shape, dt=F32):
        return self.ctx.enter_context(self.nc.psum_tensor(name + self.suffix, shape, dt))

    def sem(self, name):
        self.sems.append(self.nc.alloc_semaphore(name))
        return self.sems[-1]

    def free_semaphores(self):
        self.nc.clear_and_free_semaphores(self.sems)
        self.nc.all_engine_barrier()


def sems(m, prefix, names):
    return {n: m.sem(f"{prefix}_{n}") for n in names.split()}


def layernorm_stats(nc, m, name, x, mean_var, rstd, t0=0, t1=T):
    with ExitStack() as ctx, nc.Block() as block:
        layernorm_stats_in(block, Mem(nc, ctx), m, name, x, mean_var, rstd, t0, t1)


def layernorm_stats_in(block, l, m, name, x, mean_var, rstd, t0=0, t1=T, loaded=None, again=None):
    stats = l.sb(f"{name}_stats", [P, T, 6])
    var_eps = l.sb(f"{name}_vareps", [P, 2, T])
    std = l.sb(f"{name}_std", [P, 2, T])
    d = sems(m, name, "stats_done aggr_done eps_added std_done rstd_done half_done var_done inv_done")

    @block.vector
    def _(dve):
        for t in range(t0, t1):
            if loaded is not None and t % 4 == 0:
                dve.wait_ge(loaded[t // 4], 16)
            dve.bn_stats(stats[:, t, :], x[:, t, :]).then_inc(d["stats_done"], 1)
        for t in range(t0, t1):
            dve.wait_ge(d["stats_done"], t - t0 + 1)
            dve.bn_aggr(mean_var[:, t, :], stats[:, t, :]).then_inc(d["aggr_done"], 1)
        dve.wait_ge(d["aggr_done"], t1 - t0)
        var = mean_var[:, t0:t1, 1]
        dve.tensor_scalar(var_eps[:, 0, t0:t1], var, LN_EPS, None, ALU.add).then_inc(d["eps_added"], 1)
        dve.wait_ge(d["std_done"], 1)
        dve.reciprocal(rstd[:, t0:t1], std[:, 0, t0:t1]).then_inc(d["rstd_done"], 1)
        if again is not None:
            dve.wait_ge(d["rstd_done"], 1)
            dve.tensor_tensor(again[:, :], var, rstd[:, :], ALU.mult).then_inc(d["half_done"], 1)
            dve.wait_ge(d["half_done"], 1)
            dve.tensor_tensor(again[:, :], again[:, :], rstd[:, :], ALU.mult).then_inc(d["var_done"], 1)
            dve.wait_ge(d["var_done"], 1)
            dve.tensor_scalar(var_eps[:, 1, :], again[:, :], LN_EPS, None, ALU.add).then_inc(d["eps_added"], 1)
            dve.wait_ge(d["std_done"], 2)
            dve.reciprocal(var_eps[:, 0, :], std[:, 1, :]).then_inc(d["inv_done"], 1)
            dve.wait_ge(d["inv_done"], 1)
            dve.tensor_tensor(rstd[:, :], rstd[:, :], var_eps[:, 0, :], ALU.mult)

    @block.scalar
    def _(act):
        act.wait_ge(d["eps_added"], 1)
        act.activation(std[:, 0, t0:t1], var_eps[:, 0, t0:t1], ACT.Sqrt).then_inc(d["std_done"], 1)
        if again is not None:
            act.wait_ge(d["eps_added"], 2)
            act.activation(std[:, 1, :], var_eps[:, 1, :], ACT.Sqrt).then_inc(d["std_done"], 1)


def three_passes(pe, out, terms):
    n = 0
    for a_head, a_rest, b_head, b_rest in terms:
        for a, b in ((a_head, b_head), (a_head, b_rest), (a_rest, b_head)):
            i = pe.matmul(out, a, b, start=n == 0, stop=n == 3 * len(terms) - 1)
            n += 1
    return i


def split_weights(nc, m, name, weights):
    headed, resting = m.sem(f"{name}_headed"), m.sem(f"{name}_rest")
    with nc.Block() as block:

        @block.scalar
        def _(act):
            for whole, head, _ in weights:
                for k in range(whole.shape[1]):
                    act.activation(head[:, k, :], whole[:, k, :], ACT.Copy).then_inc(headed, 1)

        @block.vector
        def _(dve):
            n = 0
            for whole, head, rest in weights:
                for k in range(whole.shape[1]):
                    n += 1
                    dve.wait_ge(headed, n)
                    dve.tensor_tensor(rest[:, k, :], whole[:, k, :], head[:, k, :], ALU.subtract).then_inc(resting, 1)


def constants(nc, m, c, zero):
    zeroed, made, copied = m.sem("const_zeroed"), m.sem("const_made"), m.sem("const_copied")
    with nc.Block() as block:

        @block.gpsimd
        def _(pool):
            pool.memset(c.ident[:, :], 0.0).then_inc(zeroed, 1)
            pool.memset(c.mask_kq[:, :], 0.0).then_inc(zeroed, 1)
            pool.memset(c.mask_qk[:, :], 0.0).then_inc(zeroed, 1)
            pool.wait_ge(zeroed, 3)
            pool.affine_select(out=c.ident[:, :], in_=c.ident[:, :], compare_op=ALU.not_equal, fill=1.0, base=0,
                               pattern=[[-1, P]], channel_multiplier=1).then_inc(made, 1)
            pool.affine_select(out=c.mask_kq[:, :], in_=c.mask_kq[:, :], compare_op=ALU.is_ge, fill=-1e30, base=0,
                               pattern=[[1, P]], channel_multiplier=-1)
            pool.affine_select(out=c.mask_qk[:, :], in_=c.mask_qk[:, :], compare_op=ALU.is_ge, fill=-1e30, base=0,
                               pattern=[[-1, P]], channel_multiplier=1)

        @block.vector
        def _(dve):
            dve.memset(zero[:, :, :], 0.0)
            dve.memset(c.ones_row[:, :], 1.0)
            dve.memset(c.ones3[:, :], 1.0)
            dve.wait_ge(made, 1)
            dve.tensor_copy(c.identb[:, :], c.ident[:, :]).then_inc(copied, 1)


def meet(block, m, name):
    pe_there, act_there, dve_there = m.sem(f"{name}_pe"), m.sem(f"{name}_act"), m.sem(f"{name}_dve")

    @block.tensor
    def _(pe):
        pe.drain().then_inc(pe_there, 1)
        pe.wait_ge(act_there, 1)
        pe.wait_ge(dve_there, 1)

    @block.scalar
    def _(act):
        act.drain().then_inc(act_there, 1)
        act.wait_ge(pe_there, 1)
        act.wait_ge(dve_there, 1)

    @block.vector
    def _(dve):
        dve.drain().then_inc(dve_there, 1)
        dve.wait_ge(pe_there, 1)
        dve.wait_ge(act_there, 1)

    @block.sync
    def _(sp):
        sp.wait_ge(pe_there, 1)
        sp.wait_ge(act_there, 1)
        sp.wait_ge(dve_there, 1)


class Consts:
    def __init__(self, m):
        self.ident = m.sb("ident", [P, P])
        self.identb = m.sb("identb", [P, P], BF16)
        self.mask_kq = m.sb("mask_kq", [P, P], BF16)
        self.mask_qk = m.sb("mask_qk", [P, P], BF16)
        self.ones_row = m.sb("ones_row", [1, P])
        self.ones3 = m.sb("ones3", [3, P], BF16)


def l0_weights(block, nc, m, c, a, w_qkv, bias_qkv, g_h, b_h, rot):
    with ExitStack() as ctx:
        l = Mem(nc, ctx)
        raw = l.sb("w_qkv_raw", [P, DK, 3 * D])
        gain = l.sb("ln_gain", [P, 2, DK])
        shift = l.sb("ln_shift", [P, 2, DK])
        bias_in = l.sb("bias_in", [1, 3 * D])
        bias_ps = l.ps("bias_ps", [P, 2, 512])
        loaded, scaled, biased = m.sem("w0_loaded"), m.sem("w0_scaled"), m.sem("w0_biased")

        @block.sync
        def _(sp):
            sp.dma_start(raw[:, :, 0:D], a["L0_attn_Wq"].rearrange("(k p) n -> p k n", p=P)).then_inc(loaded, 16)
            sp.dma_start(raw[:, :, D:3 * D], a["L0_attn_Wkv"].rearrange("(k p) n -> p k n", p=P)
                         ).then_inc(loaded, 16)
            sp.dma_start(bias_in[0:1, 0:D], a["L0_attn_bq"][None, :]).then_inc(loaded, 16)
            sp.dma_start(bias_in[0:1, D:3 * D], a["L0_attn_bkv"][None, :]).then_inc(loaded, 16)
            sp.dma_start(rot[:, :, :, :], a["rot_table"]).then_inc(loaded, 16)

        @block.scalar
        def _(act):
            with nc.allow_non_contiguous_dma(reason="1 KB of per-feature vectors onto partitions"):
                for i, n in enumerate(("q", "kv")):
                    act.dma_start(gain[:, i, :], a[f"L0_attn_ln_{n}_g"].rearrange("(k p) -> p k", p=P)
                                  ).then_inc(loaded, 16)
                    act.dma_start(shift[:, i, :], a[f"L0_attn_ln_{n}_b"].rearrange("(k p) -> p k", p=P)
                                  ).then_inc(loaded, 16)
            act.dma_start(g_h[:, :], a["L0_attn_ln_h_g"][None, :].partition_broadcast(P)).then_inc(loaded, 16)
            act.dma_start(b_h[:, :], a["L0_attn_ln_h_b"][None, :].partition_broadcast(P)).then_inc(loaded, 16)

        @block.vector
        def _(dve):
            dve.wait_ge(loaded, 16 * 11)
            for k in range(DK):
                dve.tensor_scalar(w_qkv[:, k, 0:D], raw[:, k, 0:D], gain[:, 0, k:k + 1], None, ALU.mult)
                dve.tensor_scalar(w_qkv[:, k, D:3 * D], raw[:, k, D:3 * D], gain[:, 1, k:k + 1], None, ALU.mult)
            dve.wait_ge(biased, 1)
            dve.tensor_tensor(bias_qkv[0:1, 0:512], bias_ps[0:1, 0, :], bias_in[0:1, 0:512], ALU.add)
            dve.tensor_tensor(bias_qkv[0:1, 512:768], bias_ps[0:1, 1, 0:256], bias_in[0:1, 512:768], ALU.add)

        @block.tensor
        def _(pe):
            pe.wait_ge(loaded, 16 * 11)
            for k in range(DK):
                f, e = k == 0, k == DK - 1
                pe.matmul(bias_ps[0:1, 0, 0:256], shift[:, 0, k:k + 1], raw[:, k, 0:256], start=f, stop=e)
            for k in range(DK):
                f, e = k == 0, k == DK - 1
                pe.matmul(bias_ps[0:1, 0, 256:512], shift[:, 1, k:k + 1], raw[:, k, 256:512], start=f, stop=e)
            for k in range(DK):
                f, e = k == 0, k == DK - 1
                last = pe.matmul(bias_ps[0:1, 1, 0:256], shift[:, 1, k:k + 1], raw[:, k, 512:768],
                                 start=f, stop=e)
            last.then_inc(biased, 1)


def l0_project(nc, m, c, x, mean_var, rstd, norm_var, slots, zero, cleared, w_qkv, bias_qkv, g_h, b_h, rot, qT, kT, v):
    NH = 2 * H0
    with ExitStack() as ctx:
        l = Mem(nc, ctx)
        xh = l.sb("xh", [P, D])
        xhT = l.sb("xhT", [P, 2, DK, P])
        own = l.sb("rot_own", [P, 2, NH, HD])
        oth = l.sb("rot_oth", [P, 2, NH, HD])
        val = l.sb("val", [P, 2, NH, HD])
        rest = l.sb("rest", [P, NH, HD])
        hsum = l.sb("hsum", [P, 2, NH])
        hvar = l.sb("hvar", [P, 2, NH])
        hstd = l.sb("hstd", [P, 2, NH])
        msq = norm_var
        mroot = l.sb("mroot", [P, T])
        stack = l.sb("stack", [P, 2, NH, ROWS0], BF16)
        xT_ps = l.ps("xT_ps", [P, 2, 512])
        qkv_ps = l.ps("qkv_ps", [P, 2, 512])
        turn_ps = l.ps("turn_ps", [P, 4, 8, P], BF16)

        (xh_done, xT_done, xhT_done, qkv_done, qk_read, v_read, msq_done, mroot_done, own_done, oth_done, rot_done, sum_done,
         mean_done, cen_done, sq_done, sqs_done, var_done, std_done, inv_done, gain_done, unit_done, val_done,
         p1_done, r1_done, p2_done, p3_done, dup_done, turned, evacuated, ones_done, p12_done) = (m.sem(f"pr_{s}") for s in (
             "xh_done", "xT_done", "xhT_done", "qkv_done", "qk_read", "v_read", "msq_done", "mroot_done", "own_done", "oth_done",
             "rot_done", "sum_done", "mean_done", "cen_done", "sq_done", "sqs_done", "var_done", "std_done",
             "inv_done", "gain_done", "unit_done", "val_done", "p1_done", "r1_done", "p2_done", "p3_done",
             "dup_done", "turned", "evacuated", "ones_done", "p12_done"))

        def bc(ap, n):
            return ap.unsqueeze(2).to_broadcast([P, NH, n])

        v_ones = m.sem("pr_v_ones")


        def steps(eng, step):
            for t in range(3):
                step(t, t % 2, None)
            with eng.Fori(1, TB // 2 - 1) as pair:
                step(pair * 2 + 1, 1, 0)
                step(pair * 2 + 2, 0, 0)
            for t in range(TB - 1, TB + 3):
                step(t, t % 2, None)
            with eng.Fori(TB // 2 + 1, T // 2 - 2) as pair:
                step(pair * 2 + 1, 1, 1)
                step(pair * 2 + 2, 0, 1)
            for t in range(T - 3, T):
                step(t, t % 2, None)

        with nc.Block() as block:
            clear_slots(block, slots, zero, cleared)

            @block.vector
            def _(dve):
                for u in range(2):
                    dve.memset(stack[:, u, :, QK0:ROWS0], 1.0).then_inc(ones_done, 1)
                dve.tensor_scalar(msq[:, :], norm_var[:, :], D / 4.0, None, ALU.mult).then_inc(msq_done, 1)
                dve.wait_ge(msq_done, 1)

                def normalise(t, u):
                    reuse(dve, xT_done, t, 1)
                    dve.tensor_scalar(xh[:, :], x[:, t, :], mean_var[:, t, 0:1], rstd[:, bass.ds(t, 1)],
                                      ALU.subtract, ALU.mult).then_inc(xh_done, 1)

                def rotate(t, u, b):
                    qk = qkv_ps[:, 0, :].rearrange("p (h j e) -> p h j e", h=NH, e=2)
                    ownr = own[:, u, :, :]
                    othr = oth[:, u, :, :].rearrange("p h (j e) -> p h j e", e=2)
                    cos = rot[:, t - TB * b, 0, :].rearrange("p (o e) -> p o e", o=1).to_broadcast([P, NH, HD])
                    sin = rot[:, t - TB * b, 1, :].rearrange("p (j e) -> p j e", e=2)
                    dve.wait_ge(qkv_done, t + 1)
                    reuse(dve, p12_done, t, 2)
                    dve.tensor_tensor(ownr, qkv_ps[:, 0, :].rearrange("p (h e) -> p h e", h=NH), cos, ALU.mult
                                      ).then_inc(own_done, 1)
                    for e in range(2):
                        i = dve.tensor_tensor(othr[:, :, :, e], qk[:, :, :, 1 - e],
                                              sin[:, :, e].unsqueeze(1).to_broadcast([P, NH, HD // 2]), ALU.mult)
                        i.then_inc(oth_done, 1)
                    dve.wait_ge(own_done, t + 1)
                    dve.wait_ge(oth_done, 2 * t + 2)
                    dve.tensor_tensor(val[:, u], own[:, u], oth[:, u], ALU.add).then_inc(rot_done, 1)
                    dve.wait_ge(rot_done, t + 1)
                    dve.tensor_reduce(hsum[:, u, :], val[:, u], AX.X, ALU.add).then_inc(sum_done, 1)
                    dve.wait_ge(sum_done, t + 1)
                    dve.tensor_scalar(hsum[:, u, :], hsum[:, u, :], 1.0 / HD, None, ALU.mult).then_inc(mean_done, 1)
                    dve.wait_ge(mean_done, t + 1)
                    dve.tensor_tensor(own[:, u], val[:, u], bc(hsum[:, u, :], HD), ALU.subtract
                                      ).then_inc(cen_done, 1)

                def scale(t, u):
                    dve.wait_ge(sq_done, t + 1)
                    dve.tensor_reduce(hvar[:, u, :], oth[:, u], AX.X, ALU.add).then_inc(sqs_done, 1)
                    dve.wait_ge(sqs_done, t + 1)
                    dve.tensor_scalar(hvar[:, u, :], hvar[:, u, :], 1.0 / HD, msq[:, bass.ds(t, 1)], ALU.mult, ALU.mult
                                      ).then_inc(var_done, 1)
                    dve.wait_ge(var_done, 2 * t + 1)
                    dve.tensor_scalar(hvar[:, u, :], hvar[:, u, :], LN_EPS, None, ALU.add).then_inc(var_done, 1)
                    if not isinstance(t, int) or t + 3 < T:
                        normalise(t + 3, 1 - u)
                    dve.wait_ge(std_done, t + 1)
                    dve.reciprocal(hstd[:, u, :], hstd[:, u, :]).then_inc(inv_done, 1)
                    dve.wait_ge(inv_done, t + 1)
                    dve.tensor_scalar(hstd[:, u, :], hstd[:, u, :], mroot[:, bass.ds(t, 1)], None, ALU.mult
                                      ).then_inc(gain_done, 1)
                    dve.wait_ge(gain_done, t + 1)
                    dve.tensor_tensor(val[:, u], own[:, u], bc(hstd[:, u, :], HD), ALU.mult).then_inc(unit_done, 1)
                    dve.wait_ge(unit_done, 2 * t + 1)
                    dve.tensor_tensor(own[:, u], val[:, u], g_h[:, :].unsqueeze(1).to_broadcast([P, NH, HD]), ALU.mult
                                      ).then_inc(unit_done, 1)
                    dve.wait_ge(unit_done, 2 * t + 2)
                    dve.tensor_tensor(val[:, u], own[:, u], b_h[:, :].unsqueeze(1).to_broadcast([P, NH, HD]), ALU.add
                                      ).then_inc(val_done, 1)
                    dve.wait_ge(p1_done, t + 1)
                    reuse(dve, p12_done, t, 1)
                    reuse(dve, p3_done, t, 1, 2)
                    dve.tensor_tensor(rest[:, :, :], val[:, u], stack[:, u, :, 0:HD], ALU.subtract).then_inc(r1_done, 1)

                def step(t, u, b):
                    if not isinstance(t, int) or t + 1 < T:
                        rotate(t + 1, 1 - u, (t + 1) // TB if b is None else b)
                    scale(t, u)

                for t in range(3):
                    normalise(t, t % 2)
                rotate(0, 0, 0)
                steps(dve, step)

            @block.gpsimd
            def _(pool):
                def parts(t, u):
                    q, k = stack[:, u, 0:H0, :], stack[:, u, H0:NH, :]

                    def slot(s, i, n=1):
                        return s[:, :, i * HD:(i + n) * HD]

                    def twice(s, i, n):
                        return slot(s, i).unsqueeze(2).to_broadcast([P, H0, n, HD])

                    ones = stack[:, u, H0:NH, QK0:QK0 + 1].to_broadcast([P, H0, HD])
                    pool.wait_ge(p1_done, t + 1)
                    pool.tensor_tensor(slot(k, 3), slot(k, 0), ones, ALU.mult)
                    pool.tensor_tensor(slot(k, 5), slot(k, 0), ones, ALU.mult)
                    pool.wait_ge(p2_done, t + 1)
                    pool.tensor_tensor(slot(q, 5), rest[:, 0:H0], slot(q, 4), ALU.subtract).then_inc(p3_done, 1)
                    pool.tensor_tensor(slot(k, 2), rest[:, H0:NH], slot(k, 4), ALU.subtract).then_inc(p3_done, 1)
                    pool.tensor_tensor(slot(k, 1), slot(k, 4), ones, ALU.mult).then_inc(dup_done, 1)

                pool.memset(v[:, :, :, :], 1.0).then_inc(v_ones, 1)
                pool.wait_ge(ones_done, 2)
                for t in (0, 1):
                    parts(t, t)
                with pool.Fori(1, T // 2) as pair:
                    t = pair * 2
                    parts(t, 0)
                    parts(t + 1, 1)

            @block.scalar
            def _(act):
                act.wait_ge(msq_done, 1)
                act.activation(mroot[:, :], msq[:, :], ACT.Sqrt).then_inc(mroot_done, 1)
                act.wait_ge(ones_done, 2)

                def turned_x(t, u):
                    act.wait_ge(xT_done, t + 1)
                    reuse(act, qkv_done, t, 2)
                    act.activation(xhT[:, u, :, :], xT_ps[:, u, 0:DK * P].rearrange("p (k n) -> p k n", k=DK),
                                   ACT.Copy).then_inc(xhT_done, 1)

                def values(b, t, u):
                    act.wait_ge(qkv_done, t + 1)
                    if isinstance(t, int) and t == 0:
                        act.wait_ge(v_ones, 1)
                    act.activation(v[:, 4 * b:4 * b + 4, t - TB * b, 0:4 * VW].rearrange(
                                       "p g (h e) -> p g h e", h=4)[:, :, :, 0:HD],
                                   qkv_ps[:, 1, 0:D].rearrange("p (g h e) -> p g h e", g=4, h=4), ACT.Copy
                                   ).then_inc(v_read, 1)

                def squares(t, u):
                    act.wait_ge(cen_done, t + 1)
                    act.activation(oth[:, u], own[:, u], ACT.Square).then_inc(sq_done, 1)

                def parts(t, u):
                    act.wait_ge(var_done, 2 * t + 2)
                    act.activation(hstd[:, u, :], hvar[:, u, :], ACT.Sqrt).then_inc(std_done, 1)
                    act.wait_ge(val_done, t + 1)
                    reuse(act, turned, t, 2, 4)
                    act.activation(stack[:, u, :, 0:HD], val[:, u], ACT.Copy).then_inc(p1_done, 1)
                    act.activation(stack[:, u, 0:H0, HD:2 * HD], val[:, u, 0:H0], ACT.Copy)
                    act.activation(stack[:, u, 0:H0, 2 * HD:3 * HD], val[:, u, 0:H0], ACT.Copy)
                    act.wait_ge(r1_done, t + 1)
                    act.activation(stack[:, u, :, 4 * HD:5 * HD], rest[:, :, :], ACT.Copy).then_inc(p2_done, 1)
                    act.activation(stack[:, u, 0:H0, 3 * HD:4 * HD], rest[:, 0:H0], ACT.Copy).then_inc(p12_done, 1)

                def evacuate(b, t, u):
                    for i in range(4):
                        act.wait_ge(turned, t * 4 + (i + 1))
                        dst = (qT if i < 2 else kT)[0:ROWS0, b, 8 * (i % 2):8 * (i % 2) + 8,
                                                    bass.ds((t - TB * b) * P, P)]
                        act.activation(dst, turn_ps[0:ROWS0, i], ACT.Copy).then_inc(evacuated, 1)

                def step(t, u, b):
                    before = (t - 2) // TB if b is None else b
                    after = (t + 1) // TB if b is None else b
                    if not isinstance(t, int) or t + 2 < T:
                        turned_x(t + 2, u)
                    if not isinstance(t, int) or t + 1 < T:
                        values(after, t + 1, 1 - u)
                        squares(t + 1, 1 - u)
                    parts(t, u)
                    if not isinstance(t, int) or t > 1:
                        evacuate(before, t - 2, u)

                turned_x(0, 0)
                turned_x(1, 1)
                values(0, 0, 0)
                squares(0, 0)
                steps(act, step)
                evacuate(1, T - 2, 0)
                evacuate(1, T - 1, 1)

            @block.tensor
            def _(pe):
                def turn_x(t, u):
                    pe.wait_ge(xh_done, t + 1)
                    reuse(pe, xhT_done, t, 2)
                    for k in range(DK):
                        i = pe.transpose(xT_ps[:, u, k * P:(k + 1) * P], xh[:, k * P:(k + 1) * P], c.ident[:, :])
                    i.then_inc(xT_done, 1)

                def project(t, u):
                    pe.wait_ge(xhT_done, t + 1)
                    reuse(pe, oth_done, t, 1, 2)
                    reuse(pe, own_done, t, 1)
                    reuse(pe, v_read, t, 1)
                    for half, w in ((0, 512), (1, 256)):
                        for k in range(DK):
                            pe.matmul(qkv_ps[:, half, 0:w], xhT[:, u, k, :], w_qkv[:, k, 512 * half:512 * half + w],
                                      start=k == 0, stop=False)
                        i = pe.matmul(qkv_ps[:, half, 0:w], c.ones_row[0:1, :],
                                      bias_qkv[0:1, 512 * half:512 * half + w], start=False, stop=True)
                    i.then_inc(qkv_done, 1)

                def turn_stack(t, u):
                    pe.wait_ge(p3_done, 2 * t + 2)
                    pe.wait_ge(dup_done, t + 1)
                    pe.wait_ge(p12_done, t + 1)
                    for bank in range(4):
                        if not (isinstance(t, int) and t == 0):
                            pe.wait_ge(evacuated, t * 4 + (bank - 3))
                        for h in range(8 * bank, 8 * bank + 8):
                            i = pe.transpose(turn_ps[0:ROWS0, bank, h % 8, :], stack[:, u, h, :], c.identb[:, :])
                        i.then_inc(turned, 1)

                def step(t, u, b):
                    if not isinstance(t, int) or t + 2 < T:
                        project(t + 2, u)
                    if not isinstance(t, int) or t + 3 < T:
                        turn_x(t + 3, 1 - u)
                    if not isinstance(t, int) or t > 0:
                        turn_stack(t - 1, 1 - u)

                turn_x(0, 0)
                turn_x(1, 1)
                project(0, 0)
                turn_x(2, 0)
                project(1, 1)
                steps(pe, step)
                turn_stack(T - 1, 1)


def l0_attend(nc, m, c, qT, kT, v, att):
    NU = 64
    FREE_S, FREE_W, FREE_O, FREE_T = 4, 2, 1, 2
    with ExitStack() as ctx:
        l = Mem(nc, ctx)
        half_max = l.sb("half_max", [P, 4, TB, 2])
        row_max = l.sb("row_max", [P, 4, TB])
        rest = l.sb("max_rest", [P, 4, TB])
        shift = l.sb("max_parts", [P, 4, TB, 3], BF16)
        v_now = l.sb("v_now", [P, TB, VG])
        w = l.sb("weights", [P, 8, 512])
        outT = l.sb("outT", [P, 2, 512])
        rsum = l.sb("rsum", [P, 4, 4])
        s_ps = l.ps("s_ps", [P, 4, 512])
        m_ps = l.ps("m_ps", [P, 2, 512])
        o_ps = l.ps("o_ps", [P, 512])
        t_ps = l.ps("t_ps", [P, 512])
        t_bf = t_ps[:, :].bitcast(BF16).rearrange("p (i n) -> p i n", n=P)

        (s_done, m_done, max_done, w_done, pv_done, v_staged, comb_done, neg_done, r_done, parts_done, shT_done,
         sh_copied, o_copied, oT_done, rsum_done, att_done) = (m.sem(f"at_{s}") for s in (
             "s_done", "m_done", "max_done", "w_done", "pv_done", "v_staged", "comb_done", "neg_done", "r_done",
             "parts_done", "shT_done", "sh_copied", "o_copied", "oT_done", "rsum_done", "att_done"))

        q_g = qT[:, :, :, :].rearrange("p b (g h) n -> p (b g) h n", h=4)
        k_g = kT[:, :, :, :].rearrange("p b (g h) n -> p (b g) h n", h=4)

        with nc.Block() as block:

            @block.tensor
            def _(pe):
                def row_scores(g, u):
                    j, qt, kh = u // 16, u // 2 % 8, u % 2
                    if not (isinstance(g, int) and g == 0 and u < 2):
                        pe.wait_ge(max_done, g * NU + (u - 1))
                    pe.matmul(m_ps[:, u % 2, :], q_g[0:QK0, g, j, qt * P:(qt + 1) * P],
                              k_g[0:QK0, g, j, kh * 512:(kh + 1) * 512], start=True, stop=True).then_inc(m_done, 1)

                def turn_shift(g, j):
                    pe.wait_ge(parts_done, 4 * g + (j + 1))
                    if j == 2 and not (isinstance(g, int) and g == 0):
                        pe.wait_ge(att_done, g * 2 - 1)
                    if not (isinstance(g, int) and g == 0 and j == 0):
                        pe.wait_ge(sh_copied, 4 * g + j)
                    for qt in range(TB):
                        i = pe.transpose(t_bf[96:99, qt, :], shift[:, j, qt, :], c.identb[:, :])
                    i.then_inc(shT_done, 1)

                def scores(g, s, j):
                    qh, kt = s // 8, s % 8
                    n = g * NU + (4 * s + j)
                    if s == 0:
                        pe.wait_ge(sh_copied, 4 * g + (j + 1))
                    pe.wait_ge(w_done, FREE_S + n - 3)
                    pe.matmul(s_ps[:, j, :], k_g[0:ROWS0, g, j, kt * P:(kt + 1) * P],
                              q_g[0:ROWS0, g, j, qh * 512:(qh + 1) * 512], start=True, stop=True
                              ).then_inc(s_done, 1)

                def outputs(g, s):
                    qh, kt = s // 8, s % 8
                    pe.wait_ge(w_done, g * NU + (FREE_S + 4 * s + 4))
                    if qh == 0:
                        pe.wait_ge(v_staged, g * TB + (kt + 1))
                    if kt == 0:
                        pe.wait_ge(o_copied, g * 2 + (FREE_O + qh))
                    for j in range(4):
                        i = pe.matmul(o_ps[32 * j:32 * j + 32, :], v_now[:, kt, VW * j:VW * j + 32],
                                      w[:, s % 2 * 4 + j, :], start=kt == 0, stop=kt == TB - 1,
                                      skip_group_check=True)
                    i.then_inc(pv_done, 1)

                def turn_outputs(g, qh):
                    pe.wait_ge(o_copied, g * 2 + (FREE_O + qh + 1))
                    for i in range(4):
                        x = pe.transpose(t_ps[:, i * P:(i + 1) * P], outT[:, qh, i * P:(i + 1) * P], c.ident[:, :])
                    x.then_inc(oT_done, 1)

                def group(g, ahead):
                    for s in range(16):
                        for j in range(4):
                            scores(g, s, j)
                            if ahead:
                                row_scores(g + 1, 4 * s + j)
                        if s > 0:
                            outputs(g, s - 1)
                        if ahead and s in (5, 9, 13):
                            turn_shift(g + 1, s // 4 - 1)
                        if s == 11:
                            if ahead:
                                pe.wait_ge(sh_copied, 4 * g + 6)
                            else:
                                pe.wait_ge(att_done, 2 * g)
                            turn_outputs(g, 0)
                    outputs(g, 15)
                    if ahead:
                        turn_shift(g + 1, 3)
                        pe.wait_ge(sh_copied, 4 * g + 8)
                    else:
                        pe.wait_ge(att_done, 2 * g + 1)
                    turn_outputs(g, 1)

                pe.sem_inc(pv_done, FREE_W)
                pe.sem_inc(oT_done, FREE_T)
                for u in range(NU):
                    row_scores(0, u)
                for j in range(4):
                    turn_shift(0, j)
                with pe.Fori(0, NG - 1) as g:
                    group(g, True)
                group(NG - 1, False)

            @block.vector
            def _(dve):
                def maximum(g, u):
                    dve.wait_ge(m_done, g * NU + (u + 1))
                    dve.tensor_reduce(half_max[:, u // 16, u // 2 % 8, u % 2:u % 2 + 1], m_ps[:, u % 2, :], AX.X,
                                      ALU.max).then_inc(max_done, 1)

                def parts(g, j):
                    n = 4 * g + j
                    dve.wait_ge(max_done, g * NU + 16 * (j + 1))
                    dve.tensor_reduce(row_max[:, j, :], half_max[:, j, :, :], AX.X, ALU.max).then_inc(comb_done, 1)
                    dve.wait_ge(comb_done, n + 1)
                    if not (isinstance(g, int) and g == 0):
                        dve.wait_ge(shT_done, n - 3)
                    dve.tensor_scalar(shift[:, j, :, 0], row_max[:, j, :], -1.0, None, ALU.mult
                                      ).then_inc(neg_done, 1)
                    dve.wait_ge(neg_done, n + 1)
                    dve.scalar_tensor_tensor(rest[:, j, :], row_max[:, j, :], -1.0, shift[:, j, :, 0], ALU.mult,
                                             ALU.subtract).then_inc(r_done, 1)
                    dve.wait_ge(r_done, 2 * n + 1)
                    dve.tensor_copy(shift[:, j, :, 1], rest[:, j, :]).then_inc(r_done, 1)
                    dve.wait_ge(r_done, 2 * n + 2)
                    dve.tensor_tensor(shift[:, j, :, 2], rest[:, j, :], shift[:, j, :, 1], ALU.subtract
                                      ).then_inc(parts_done, 1)

                def normalise(g, qh):
                    x = t_ps[:, :].rearrange("p (q h e) -> p q h e", q=4, h=4)
                    dve.wait_ge(oT_done, g * 2 + (FREE_T + qh + 1))
                    dve.reciprocal(rsum[:, :, :], x[:, :, :, HD]).then_inc(rsum_done, 1)
                    dve.wait_ge(rsum_done, g * 2 + (qh + 1))
                    dve.tensor_tensor(att[:, g, 4 * qh:4 * qh + 4, :].rearrange("p q (h e) -> p q h e", h=4),
                                      x[:, :, :, 0:HD], rsum[:, :, :].unsqueeze(3).to_broadcast([P, 4, 4, HD]),
                                      ALU.mult).then_inc(att_done, 1)

                def group(g, ahead):
                    for s in range(16):
                        if ahead:
                            for j in range(4):
                                maximum(g + 1, 4 * s + j)
                            if s % 4 == 3:
                                parts(g + 1, s // 4)
                        if s == 12:
                            normalise(g, 0)
                    normalise(g, 1)

                for u in range(NU):
                    maximum(0, u)
                    if u % 16 == 15:
                        parts(0, u // 16)
                with dve.Fori(0, NG - 1) as g:
                    group(g, True)
                group(NG - 1, False)

            @block.scalar
            def _(act):
                def weights(g, s):
                    for j in range(4):
                        act.wait_ge(s_done, g * NU + (4 * s + j + 1))
                        if j == 0:
                            act.wait_ge(pv_done, g * 16 + (FREE_W + s - 1))
                        act.activation(w[:, s % 2 * 4 + j, :], s_ps[:, j, :], ACT.Exp, scale=HD ** -0.5
                                       ).then_inc(w_done, 1)

                def place_shift(g, j):
                    act.wait_ge(shT_done, 4 * g + (j + 1))
                    act.activation(q_g[QK0:ROWS0, g, j, :], t_bf[96:99, :, :], ACT.Copy).then_inc(sh_copied, 1)

                def copy_out(g, qh):
                    act.wait_ge(pv_done, g * 16 + (FREE_W + 8 * qh + 8))
                    act.wait_ge(oT_done, g * 2 + (FREE_T + qh - 1))
                    act.activation(outT[:, qh, :], o_ps[:, :], ACT.Copy).then_inc(o_copied, 1)

                def group(g, ahead):
                    for s in range(16):
                        weights(g, s)
                        if s == 8:
                            copy_out(g, 0)
                        if ahead and s in (5, 9, 13):
                            place_shift(g + 1, s // 4 - 1)
                    copy_out(g, 1)
                    if ahead:
                        place_shift(g + 1, 3)

                act.sem_inc(w_done, FREE_S)
                act.sem_inc(o_copied, FREE_O)
                for j in range(4):
                    place_shift(0, j)
                with act.Fori(0, NG - 1) as g:
                    group(g, True)
                group(NG - 1, False)

            @block.gpsimd
            def _(pool):
                def stage(g, kt):
                    if not (isinstance(g, int) and g == 0):
                        pool.wait_ge(pv_done, g * 16 + (FREE_W + kt - 7))
                    pool.tensor_copy(v_now[:, kt, :], v[:, g, kt, :]).then_inc(v_staged, 1)

                for kt in range(TB):
                    stage(0, kt)
                with pool.Fori(1, NG) as g:
                    for kt in range(TB):
                        stage(g, kt)


def l0_output(nc, m, c, a, att, x_dram, x):
    with ExitStack() as ctx:
        l = Mem(nc, ctx)
        attT = l.sb("attT", [P, 2, DK, P])
        turn_ps = l.ps("attT_ps", [P, 2, 512])
        y_ps = l.ps("y_ps", [P, 2, 512])
        w_o = l.sb("w_o", [P, DK, D])
        bias_o = l.sb("bias_o", [1, D])
        att_now = l.sb("att_now", [P, 2, D])
        joined, turned, copied, y_done, added, w_loaded, x_loaded = (m.sem(f"l0o_{s}") for s in (
            "joined", "turned", "copied", "y_done", "added", "w_loaded", "x_loaded"))
        with nc.Block() as block:

            @block.sync
            def _(sp):
                sp.dma_start(w_o[:, :, :], a["L0_attn_Wo"].rearrange("(k p) n -> p k n", p=P)).then_inc(w_loaded, 16)
                sp.dma_start(bias_o[0:1, :], a["L0_attn_bo"][None, :]).then_inc(w_loaded, 16)
                sp.dma_start(x[:, :, :], x_dram).then_inc(x_loaded, 16)

            @block.gpsimd
            def _(pool):
                for t in range(T):
                    reuse(pool, turned, t, 2)
                    g = t // TB * 4
                    pool.tensor_scalar(att_now[:, t % 2, :].rearrange("p (g n) -> p g n", g=4),
                                       att[:, g:g + 4, t % TB, :], 1.0, None, ALU.mult).then_inc(joined, 1)

            @block.tensor
            def _(pe):
                def turn(t):
                    reuse(pe, copied, t, 2)
                    pe.wait_ge(joined, t + 1)
                    for k in range(DK):
                        i = pe.transpose(turn_ps[:, t % 2, k * P:(k + 1) * P], att_now[:, t % 2, k * P:(k + 1) * P],
                                         c.ident[:, :])
                    i.then_inc(turned, 1)

                turn(0)
                pe.wait_ge(w_loaded, 32)
                for t in range(T):
                    if t + 1 < T:
                        turn(t + 1)
                    pe.wait_ge(copied, t + 1)
                    reuse(pe, added, t, 2)
                    for k in range(DK):
                        pe.matmul(y_ps[:, t % 2, 0:D], attT[:, t % 2, k, :], w_o[:, k, :], start=k == 0, stop=False)
                    pe.matmul(y_ps[:, t % 2, 0:D], c.ones_row[0:1, :], bias_o[0:1, :], start=False, stop=True
                              ).then_inc(y_done, 1)

            @block.scalar
            def _(act):
                for t in range(T):
                    act.wait_ge(turned, t + 1)
                    reuse(act, y_done, t, 2)
                    act.activation(attT[:, t % 2], turn_ps[:, t % 2, 0:D].rearrange("p (k n) -> p k n", k=DK),
                                   ACT.Copy).then_inc(copied, 1)

            @block.vector
            def _(dve):
                dve.wait_ge(x_loaded, 16)
                for t in range(T):
                    dve.wait_ge(y_done, t + 1)
                    dve.tensor_tensor(x[:, t, :], x[:, t, :], y_ps[:, t % 2, 0:D], ALU.add).then_inc(added, 1)


def normalise_all(nc, m, name, x, mean_var, rstd, out):
    with nc.Block() as block:

        @block.vector
        def _(dve):
            for t in range(T):
                dve.tensor_scalar(out[:, t, :], x[:, t, :], mean_var[:, t, 0:1], rstd[:, t:t + 1],
                                  ALU.subtract, ALU.mult)


def layer0_attention(nc, m, c, a, work, x_dram, loaded, slots, zero, cleared):
    with ExitStack() as ctx:
        l = Mem(nc, ctx)
        w_qkv = l.sb("w_qkv", [P, DK, 3 * D])
        bias_qkv = l.sb("bias_qkv", [1, 3 * D])
        g_h = l.sb("g_h", [P, HD])
        b_h = l.sb("b_h", [P, HD])
        rot = l.sb("rot", [P, TB, 2, HD])
        mean_var = l.sb("mean_var", [P, T, 2])
        rstd = l.sb("rstd", [P, T])
        norm_var = l.sb("norm_var", [P, T])
        with ExitStack() as ctx2, nc.Block() as block:
            layernorm_stats_in(block, Mem(nc, ctx2), m, "ln0", work, mean_var, rstd, loaded=loaded, again=norm_var)
            l0_weights(block, nc, m, c, a, w_qkv, bias_qkv, g_h, b_h, rot)
        qT = l.sb("qT", [P, B, H0, S], BF16)
        kT = l.sb("kT", [P, B, H0, S], BF16)
        v = l.sb("v", [P, NG, TB, VG])
        l0_project(nc, m, c, work, mean_var, rstd, norm_var, slots, zero, cleared, w_qkv, bias_qkv, g_h, b_h, rot, qT, kT, v)
        att = work[:, :, :].rearrange("p t d -> p (t d)").rearrange("p (g q n) -> p g q n", g=NG, q=TB)
        l0_attend(nc, m, c, qT, kT, v, att)
    x = m.sb("x", [P, T, D])
    l0_output(nc, m, c, a, att, x_dram, x)
    return x


NE, TOPK, FE = 64, 6, 176
FE2 = FE - P
VC = 192
WC = VC + FE
SLOTS = 256
OVER0 = NE * SLOTS
NOVER = max(k + min(13 * k, (T * P * TOPK - 257 * k) // P) for k in range(1, T * P * TOPK // 257 + 1))
ROWS = OVER0 + NOVER * P
QUAD = 4


def clear_slots(block, slots, zero, cleared):

    @block.sync
    def _(sp):
        n = ROWS // P // 8
        view = slots.rearrange("(i p n) (k d) -> i p (n k) d", p=P, n=n, k=DK)
        for i in range(8):
            sp.dma_start(view[i], zero[:, 0:1, :].to_broadcast([P, n * DK, P])).then_inc(cleared, 16)


def load_expert(eng, wgv, wo, sem, g, v, o):
    eng.dma_start(wgv[:, :, 0:FE], g.rearrange("(k p) n -> p k n", p=P)).then_inc(sem, 16)
    eng.dma_start(wgv[:, :, VC:WC], v.rearrange("(k p) n -> p k n", p=P)).then_inc(sem, 16)
    eng.dma_start(wo[:, 0, :], o[0:P, :]).then_inc(sem, 16)
    eng.dma_start(wo[0:FE2, 1, :], o[P:FE, :]).then_inc(sem, 16)


LOADS = 4 * 16


def expert_up(pe, wgv, xT, out):
    for j in range(3):
        w = min(P, WC - j * P)
        for k in range(DK):
            i = pe.matmul(out[j][0:w], wgv[:, k, j * P:j * P + w], xT[:, k, :], start=k == 0, stop=k == DK - 1)
    return i


def expert_gate(act, up, gate, sem):
    act.activation(gate[:, 0, :], up[0], ACT.Silu).then_inc(sem, 1)
    act.activation(gate[0:FE2, 1, :], up[1][0:FE2], ACT.Silu).then_inc(sem, 1)


def expert_hidden(dve, up, gate, hid):
    dve.tensor_tensor(hid[0:64, 0, :], gate[0:64, 0, :], up[1][64:P], ALU.mult)
    dve.tensor_tensor(hid[64:P, 0, :], gate[64:P, 0, :], up[2][0:64], ALU.mult)
    return dve.tensor_tensor(hid[0:FE2, 1, :], gate[0:FE2, 1, :], up[2][64:64 + FE2], ALU.mult)


def expert_down(pe, hid, wo, out, t):
    pe.matmul(out, hid[:, 0, t * P:(t + 1) * P], wo[:, 0, :], start=True, stop=False)
    return pe.matmul(out, hid[0:FE2, 1, t * P:(t + 1) * P], wo[0:FE2, 1, :], start=False, stop=True)


def moe_route(nc, m, c, a, xn, xT, slot, weight, over_table):
    CH = 4
    NCH = T // CH
    with ExitStack() as ctx:
        l = Mem(nc, ctx)
        wr_raw = l.sb("wr_raw", [NE, D])
        w_r = l.sb("w_r", [P, DK, NE])
        logits = l.sb("logits", [P, T, NE])
        top = l.sb("top", [P, T, 8])
        index = l.sb("index", [P, T, 8], U32)
        index_f = l.sb("index_f", [P, T, 8])
        shifted = l.sb("shifted", [P, T, NE])
        exps = l.sb("exps", [P, T, NE])
        esum = l.sb("esum", [P, T])
        einv = l.sb("einv", [P, T])
        top_sh = l.sb("top_sh", [P, T, TOPK])
        top_exp = l.sb("top_exp", [P, T, TOPK])
        iota_e = l.sb("iota_e", [P, NE])
        iota_k = l.sb("iota_k", [P, 16])
        iota_p = l.sb("iota_p", [P, 1])
        lower = l.sb("lower", [P, P], BF16)
        ones = l.sb("ones_moe", [P, P], BF16)
        pick = l.sb("pick", [P, TOPK, T, NE], BF16)
        pairs = l.sb("pick_pairs", [P, 3, T, NE], BF16)
        mask = l.sb("mask", [P, T, NE], BF16)
        before = l.sb("before", [P, T + 1, NE])
        rank = l.sb("rank", [P, T, NE])
        beyond = l.sb("beyond", [P, T, NE])
        place = l.sb("place", [P, T, NE])
        chosen = l.sb("chosen", [P, 2, T, NE])
        extra = l.sb("extra", [P, NE])
        over_cmp = l.sb("over_cmp", [P, NE, 16])
        tiles = l.sb("over_tiles", [P, NE])
        ends = l.sb("ends", [P, NE])
        jump = l.sb("jump", [P, NE])
        ended = l.sb("ended", [P, NE])
        owner = l.sb("owner", [P, 1])
        slot_f = l.sb("slot_f", [P, T, TOPK])
        x_ps = l.ps("xm_ps", [P, 4, 512])
        r_ps = l.ps("rt_ps", [P, 2, 512])
        n_ps = l.ps("nt_ps", [P, 2, 512])
        d = sems(m, "rt", "loaded made lower_made x_turned x_copied wr_turned wr_copied log_done log_copied top_done "
                 "index_done indf_done shift_done tsh_done exp_done texp_done esum_done einv_done pick_done pair_done "
                 "four_done mask_done rank_done tot_done before_done rank_read beyond_done extra_done cmp_done tiles_done "
                 "ends_done jump_done jumped moved place_done chosen_done slotf_done ended_done owner_done row_done")

        with nc.Block() as block:

            @block.sync
            def _(sp):
                sp.dma_start(wr_raw[:, :], a["L0_ffn_w_router"]).then_inc(d["loaded"], 16)

            @block.gpsimd
            def _(pool):
                pool.iota(iota_e[:, :], [[1, NE]], base=0, channel_multiplier=0,
                          allow_small_or_imprecise_dtypes=True).then_inc(d["made"], 1)
                pool.iota(iota_k[:, :], [[P, 16]], base=0, channel_multiplier=0,
                          allow_small_or_imprecise_dtypes=True).then_inc(d["made"], 1)
                pool.iota(iota_p[:, :], [[0, 1]], base=0, channel_multiplier=1,
                          allow_small_or_imprecise_dtypes=True).then_inc(d["made"], 1)
                pool.memset(ones[:, :], 1.0).then_inc(d["made"], 1)
                pool.memset(before[:, 0, :], 0.0).then_inc(d["made"], 1)
                pool.memset(lower[:, :], 1.0).then_inc(d["lower_made"], 1)
                pool.wait_ge(d["lower_made"], 1)
                pool.affine_select(out=lower[:, :], in_=lower[:, :], compare_op=ALU.is_gt, fill=0.0, base=0,
                                   pattern=[[1, P]], channel_multiplier=-1).then_inc(d["made"], 1)

            @block.tensor
            def _(pe):
                pe.wait_ge(d["loaded"], 16)
                for k in range(DK):
                    i = pe.transpose(r_ps[:, 1, k * NE:(k + 1) * NE], wr_raw[:, k * P:(k + 1) * P],
                                     c.ident[0:NE, 0:NE])
                i.then_inc(d["wr_turned"], 1)
                for ch in range(NCH):
                    for k in range(DK):
                        reuse(pe, d["x_copied"], ch * DK + k, 4)
                        for t in range(CH):
                            i = pe.transpose(x_ps[:, (ch * DK + k) % 4, t * P:(t + 1) * P],
                                             xn[:, ch * CH + t, k * P:(k + 1) * P], c.ident[:, :])
                        i.then_inc(d["x_turned"], 1)
                pe.wait_ge(d["wr_copied"], 1)
                for ch in range(NCH):
                    pe.wait_ge(d["x_copied"], DK * (ch + 1))
                    reuse(pe, d["log_copied"], ch, 2)
                    for t in range(ch * CH, ch * CH + CH):
                        for k in range(DK):
                            i = pe.matmul(r_ps[:, ch % 2, t % CH * NE:(t % CH + 1) * NE], xT[:, k, t * P:(t + 1) * P],
                                          w_r[:, k, :], start=k == 0, stop=k == DK - 1)
                    i.then_inc(d["log_done"], 1)
                pe.wait_ge(d["made"], 6)
                pe.wait_ge(d["log_copied"], NCH)
                pe.wait_ge(d["mask_done"], 1)
                for h in range(2):
                    half = mask[:, 8 * h:8 * h + 8, :].rearrange("p t e -> p (t e)")
                    pe.matmul(n_ps[:, h, :], ones[:, :], half, start=True, stop=True).then_inc(d["tot_done"], 1)
                for h in range(2):
                    half = mask[:, 8 * h:8 * h + 8, :].rearrange("p t e -> p (t e)")
                    pe.matmul(r_ps[:, h, :], lower[:, :], half, start=True, stop=True).then_inc(d["rank_done"], 1)
                pe.wait_ge(d["owner_done"], 2)
                pe.matmul(x_ps[0:1, 0, 0:P], owner[:, 0:1], c.ident[:, :], start=True, stop=True
                          ).then_inc(d["row_done"], 1)

            @block.scalar
            def _(act):
                act.wait_ge(d["wr_turned"], 1)
                act.activation(w_r[:, :, :], r_ps[:, 1, 0:DK * NE].rearrange("p (k e) -> p k e", k=DK), ACT.Copy
                               ).then_inc(d["wr_copied"], 1)
                for ch in range(NCH):
                    for k in range(DK):
                        act.wait_ge(d["x_turned"], DK * ch + k + 1)
                        act.activation(xT[:, k, ch * 512:(ch + 1) * 512], x_ps[:, (ch * DK + k) % 4, :], ACT.Copy
                                       ).then_inc(d["x_copied"], 1)
                act.wait_ge(d["shift_done"], 1)
                act.activation(exps[:, :, :], shifted[:, :, :], ACT.Exp).then_inc(d["exp_done"], 1)
                act.wait_ge(d["tsh_done"], 1)
                act.activation(top_exp[:, :, :], top_sh[:, :, :], ACT.Exp).then_inc(d["texp_done"], 1)

            @block.vector
            def _(dve):
                def over_e(ap):
                    return ap.unsqueeze(2).to_broadcast([P, T, NE])

                def over_t(ap):
                    return ap.unsqueeze(1).to_broadcast([P, T, NE])

                for ch in range(NCH):
                    dve.wait_ge(d["log_done"], ch + 1)
                    dve.tensor_copy(logits[:, ch * CH:(ch + 1) * CH, :],
                                    r_ps[:, ch % 2, 0:CH * NE].rearrange("p (t e) -> p t e", t=CH)
                                    ).then_inc(d["log_copied"], 1)
                    dve.wait_ge(d["log_copied"], ch + 1)
                    for t in range(ch * CH, (ch + 1) * CH):
                        dve.max(top[:, t, :], logits[:, t, :]).then_inc(d["top_done"], 1)
                    for t in range(ch * CH, (ch + 1) * CH):
                        dve.wait_ge(d["top_done"], t + 1)
                        dve.max_index(index[:, t, :], top[:, t, :], logits[:, t, :]).then_inc(d["index_done"], 1)
                dve.wait_ge(d["index_done"], T)
                dve.tensor_copy(index_f[:, :, :], index[:, :, :]).then_inc(d["indf_done"], 1)
                dve.tensor_tensor(shifted[:, :, :], logits[:, :, :], over_e(top[:, :, 0]), ALU.subtract
                                  ).then_inc(d["shift_done"], 1)
                dve.tensor_tensor(top_sh[:, :, :], top[:, :, 0:TOPK],
                                  top[:, :, 0:1].to_broadcast([P, T, TOPK]), ALU.subtract).then_inc(d["tsh_done"], 1)
                dve.wait_ge(d["made"], 6)
                dve.wait_ge(d["indf_done"], 1)
                for j in range(TOPK):
                    dve.tensor_tensor(pick[:, j], over_t(iota_e[:, :]), over_e(index_f[:, :, j]), ALU.is_equal
                                      ).then_inc(d["pick_done"], 1)
                for j in range(3):
                    dve.wait_ge(d["pick_done"], 2 * j + 2)
                    dve.tensor_tensor(pairs[:, j], pick[:, 2 * j], pick[:, 2 * j + 1], ALU.add).then_inc(d["pair_done"], 1)
                dve.wait_ge(d["pair_done"], 3)
                dve.tensor_tensor(pairs[:, 0], pairs[:, 0], pairs[:, 1], ALU.add).then_inc(d["four_done"], 1)
                dve.wait_ge(d["four_done"], 1)
                dve.tensor_tensor(mask[:, :, :], pairs[:, 0], pairs[:, 2], ALU.add).then_inc(d["mask_done"], 1)
                dve.wait_ge(d["exp_done"], 1)
                dve.tensor_reduce(esum[:, :], exps[:, :, :], AX.X, ALU.add).then_inc(d["esum_done"], 1)
                dve.wait_ge(d["esum_done"], 1)
                dve.reciprocal(einv[:, :], esum[:, :]).then_inc(d["einv_done"], 1)
                dve.wait_ge(d["einv_done"], 1)
                dve.wait_ge(d["texp_done"], 1)
                dve.tensor_tensor(weight[:, :, :], top_exp[:, :, :], einv[:, :].unsqueeze(2).to_broadcast([P, T, TOPK]),
                                  ALU.mult)
                for t in range(T):
                    dve.wait_ge(d["tot_done"], t // 8 + 1)
                    if t:
                        dve.wait_ge(d["before_done"], t)
                    dve.tensor_tensor(before[:, t + 1, :], before[:, t, :], n_ps[:, t // 8, t % 8 * NE:(t % 8 + 1) * NE],
                                      ALU.add).then_inc(d["before_done"], 1)
                dve.wait_ge(d["before_done"], T)
                dve.tensor_scalar(extra[:, :], before[:, T, :], -float(SLOTS), None, ALU.add).then_inc(d["extra_done"], 1)
                dve.wait_ge(d["extra_done"], 1)
                dve.tensor_tensor(over_cmp[:, :, :], extra[:, :].unsqueeze(2).to_broadcast([P, NE, 16]),
                                  iota_k[:, :].unsqueeze(1).to_broadcast([P, NE, 16]), ALU.is_gt
                                  ).then_inc(d["cmp_done"], 1)
                dve.wait_ge(d["cmp_done"], 1)
                dve.tensor_reduce(tiles[:, :], over_cmp[:, :, :], AX.X, ALU.add).then_inc(d["tiles_done"], 1)
                dve.wait_ge(d["tiles_done"], 1)
                dve.tensor_tensor_scan(ends[:, :], tiles[:, :], tiles[:, :], 0.0, ALU.add, ALU.max
                                       ).then_inc(d["ends_done"], 1)
                dve.wait_ge(d["ends_done"], 1)
                dve.tensor_tensor(jump[:, :], ends[:, :], tiles[:, :], ALU.subtract).then_inc(d["jump_done"], 1)
                dve.wait_ge(d["jump_done"], 1)
                dve.tensor_scalar(jump[:, :], jump[:, :], float(P), float(OVER0 - SLOTS), ALU.mult, ALU.add
                                  ).then_inc(d["jump_done"], 1)
                dve.wait_ge(d["jump_done"], 2)
                dve.scalar_tensor_tensor(jump[:, :], iota_e[:, :], -float(SLOTS), jump[:, :], ALU.mult, ALU.add
                                         ).then_inc(d["jump_done"], 1)
                dve.tensor_scalar(ended[:, :], ends[:, :], iota_p[:, 0:1], None, ALU.is_le).then_inc(d["ended_done"], 1)
                dve.wait_ge(d["ended_done"], 1)
                dve.tensor_reduce(owner[:, :], ended[:, :], AX.X, ALU.add).then_inc(d["owner_done"], 1)
                dve.wait_ge(d["owner_done"], 1)
                dve.tensor_scalar(owner[:, :], owner[:, :], float(NE - 1), None, ALU.min).then_inc(d["owner_done"], 1)
                dve.wait_ge(d["rank_done"], 2)
                dve.tensor_tensor(rank[:, :, :], r_ps[:, :, :].rearrange("p h (t e) -> p (h t) e", e=NE),
                                  before[:, 0:T, :], ALU.add).then_inc(d["rank_read"], 1)
                dve.wait_ge(d["rank_read"], 1)
                dve.tensor_scalar(beyond[:, :, :], rank[:, :, :], float(SLOTS), None, ALU.is_ge
                                  ).then_inc(d["beyond_done"], 1)
                dve.wait_ge(d["beyond_done"], 1)
                dve.wait_ge(d["jump_done"], 3)
                dve.tensor_tensor(beyond[:, :, :], beyond[:, :, :], over_t(jump[:, :]), ALU.mult
                                  ).then_inc(d["jumped"], 1)
                dve.scalar_tensor_tensor(place[:, :, :], over_t(iota_e[:, :]), float(SLOTS), rank[:, :, :], ALU.mult,
                                         ALU.add).then_inc(d["moved"], 1)
                dve.wait_ge(d["jumped"], 1)
                dve.wait_ge(d["moved"], 1)
                dve.tensor_tensor(place[:, :, :], place[:, :, :], beyond[:, :, :], ALU.add).then_inc(d["place_done"], 1)
                dve.wait_ge(d["place_done"], 1)
                for j in range(TOPK):
                    if j >= 2:
                        dve.wait_ge(d["slotf_done"], j - 1)
                    dve.tensor_tensor(chosen[:, j % 2], pick[:, j], place[:, :, :], ALU.mult).then_inc(d["chosen_done"], 1)
                    dve.wait_ge(d["chosen_done"], j + 1)
                    dve.tensor_reduce(slot_f[:, :, j], chosen[:, j % 2], AX.X, ALU.add).then_inc(d["slotf_done"], 1)
                dve.wait_ge(d["slotf_done"], TOPK)
                dve.tensor_copy(slot[:, :, :], slot_f[:, :, :])
                dve.wait_ge(d["row_done"], 1)
                dve.tensor_copy(over_table[0:1, 0:NOVER], x_ps[0:1, 0, 0:NOVER])
                dve.tensor_copy(over_table[0:1, NOVER:NOVER + 1], ends[0:1, NE - 1:NE])


def moe_scatter(nc, m, c, a, x, xn, xT, slot, slots, cleared, prepare):
    CH = 4
    NCH = T // CH
    with nc.Block() as block, ExitStack() as ctx:
        scattered = m.sem("scattered")

        @block.gpsimd
        def _(pool):
            pool.wait_ge(cleared, 16 * 8)
            for t in range(T):
                for j in range(TOPK):
                    pool.indirect_dma_start(slots, bass.IndirectOffsetOnAxis(ap=slot[:, t, j:j + 1], axis=0),
                                            xn[:, t, :], None).then_inc(scattered, 16)
            pool.wait_ge(scattered, 16 * T * TOPK)

        prepare(block)
        meet(block, m, "prepared")

        l = Mem(nc, ctx)
        wgv = l.sb("sh_wgv", [P, DK, WC])
        wo = l.sb("sh_wo", [P, 2, D])
        gate = l.sb("sh_gate", [P, 2, 512])
        hid = l.sb("sh_hid", [P, 2, 512])
        up_ps = l.ps("shup_ps", [P, 2, 3, 512])
        y_ps = l.ps("shy_ps", [P, 2, 512])
        d = sems(m, "sh", "loaded padded up_done gate_done hid_done y_done y_added")

        @block.sync
        def _(sp):
            load_expert(sp, wgv, wo, d["loaded"], a["L0_ffn_swg"], a["L0_ffn_swv"], a["L0_ffn_swo"])

        @block.tensor
        def _(pe):
            pe.wait_ge(d["loaded"], LOADS)
            pe.wait_ge(d["padded"], 1)

            def up(ch):
                reuse(pe, d["hid_done"], ch, 2)
                expert_up(pe, wgv, xT[:, :, ch * 512:(ch + 1) * 512], [up_ps[:, ch % 2, j, :] for j in range(3)]
                          ).then_inc(d["up_done"], 1)

            up(0)
            for ch in range(NCH):
                if ch + 1 < NCH:
                    up(ch + 1)
                pe.wait_ge(d["hid_done"], ch + 1)
                for t in range(CH):
                    n = ch * CH + t
                    reuse(pe, d["y_added"], n, 2)
                    expert_down(pe, hid, wo, y_ps[:, n % 2, 0:D], t).then_inc(d["y_done"], 1)

        @block.scalar
        def _(act):
            for ch in range(NCH):
                act.wait_ge(d["up_done"], ch + 1)
                if ch:
                    act.wait_ge(d["hid_done"], ch)
                expert_gate(act, [up_ps[:, ch % 2, j, :] for j in range(3)], gate, d["gate_done"])

        @block.vector
        def _(dve):
            dve.memset(wgv[:, :, FE:VC], 0.0).then_inc(d["padded"], 1)
            for ch in range(NCH):
                dve.wait_ge(d["gate_done"], 2 * ch + 2)
                if ch:
                    dve.wait_ge(d["y_done"], ch * CH)
                expert_hidden(dve, [up_ps[:, ch % 2, j, :] for j in range(3)], gate, hid).then_inc(d["hid_done"], 1)
                for t in range(ch * CH, ch * CH + CH):
                    dve.wait_ge(d["y_done"], t + 1)
                    dve.tensor_tensor(x[:, t, :], x[:, t, :], y_ps[:, t % 2, 0:D], ALU.add).then_inc(d["y_added"], 1)


def moe_experts(nc, m, c, a, slots, wgv, wo, bufs):
    NG4 = NE // QUAD
    with ExitStack() as ctx:
        l = Mem(nc, ctx)
        rows = l.sb("rows", [P, QUAD, 2, D])
        xT = l.sb("rowsT", [P, 2, DK, SLOTS])
        gate = l.sb("ex_gate", [P, 2, 2, SLOTS])
        hid = l.sb("ex_hid", [P, 2, 2, SLOTS])
        out = l.sb("ex_out", [P, 2, 2, D])
        up_ps = l.ps("ex_up_ps", [P, 2, 3, 512])
        x_ps = l.ps("ex_x_ps", [P, DK, SLOTS])
        y_ps = l.ps("ex_y_ps", [P, 2, D])
        w_loaded = [m.sem(f"ex_w_loaded{b}") for b in range(QUAD)]
        r_loaded = [m.sem(f"ex_r_loaded{b}") for b in range(QUAD)]
        stored = [m.sem(f"ex_stored{b}") for b in range(2)]
        d = sems(m, "ex", "padded x_turned x_copied up_done gate_done hid_done y_done y_copied")
        region = slots[0:OVER0, :].rearrange("(e t p) d -> e p t d", p=P, t=2)

        def up(u):
            return [up_ps[:, u, j, 0:SLOTS] for j in range(3)]

        def rounds(eng, quad, first=0):
            quad(0)
            with eng.Fori(1, NG4 - 1) as g:
                quad(g)
            quad(NG4 - 1)

        def is_last(g):
            return isinstance(g, int) and g == NG4 - 1

        def is_first(g):
            return isinstance(g, int) and g == 0

        with nc.Block() as block:

            @block.sync
            def _(sp):
                def load(e, b):
                    sp.dma_start(rows[:, b], region[bass.ds(e, 1)].rearrange("o p t d -> p (o t) d")
                                 ).then_inc(r_loaded[b], 16)
                    load_expert(sp, wgv[:, b], wo[:, b], w_loaded[b],
                                *(a[f"L0_ffn_w{n}"][bass.ds(e, 1)].rearrange("o r n -> (o r) n") for n in "gvo"))

                def quad(g):
                    for b in range(QUAD):
                        e = g * QUAD + b
                        sp.wait_ge(d["y_copied"], e + 1)
                        sp.dma_start(region[bass.ds(e, 1)].rearrange("o p t d -> p (o t) d"), out[:, b % 2]
                                     ).then_inc(stored[b % 2], 16)
                        if not is_last(g):
                            load(e + QUAD, b)

                for b in range(QUAD):
                    load(b, b)
                rounds(sp, quad)
                for b in range(2):
                    sp.wait_ge(stored[b], 16 * NE // 2)

            @block.tensor
            def _(pe):
                def turn(g, b):
                    e = g * QUAD + b
                    if b < QUAD:
                        pe.wait_ge(r_loaded[b], g * 16 + 16)
                    else:
                        pe.wait_ge(r_loaded[0], g * 16 + 32)
                    if not (is_first(g) and b == 0):
                        pe.wait_ge(d["x_copied"], e)
                    for k in range(DK):
                        for t in range(2):
                            i = pe.transpose(x_ps[:, k, t * P:(t + 1) * P], rows[:, b % QUAD, t, k * P:(k + 1) * P],
                                             c.ident[:, :])
                    i.then_inc(d["x_turned"], 1)

                def project(g, b):
                    e = g * QUAD + b
                    pe.wait_ge(w_loaded[b], g * LOADS + LOADS)
                    pe.wait_ge(d["x_copied"], e + 1)
                    if not (is_first(g) and b < 2):
                        pe.wait_ge(d["hid_done"], e - 1)
                    expert_up(pe, wgv[:, b], xT[:, b % 2], up(b % 2)).then_inc(d["up_done"], 1)

                def down(g, b):
                    e = g * QUAD + b
                    pe.wait_ge(d["hid_done"], e + 1)
                    if not (is_first(g) and b == 0):
                        pe.wait_ge(d["y_copied"], e)
                    for t in range(2):
                        i = expert_down(pe, hid[:, b % 2], wo[:, b % QUAD], y_ps[:, t, :], t)
                    i.then_inc(d["y_done"], 1)

                def quad(g):
                    for b in range(QUAD):
                        project(g, b)
                        if not (is_last(g) and b == QUAD - 1):
                            turn(g, b + 1)
                        if not (is_first(g) and b == 0):
                            down(g, b - 1)

                pe.wait_ge(d["padded"], 1)
                turn(0, 0)
                rounds(pe, quad)
                down(NG4, -1)

            @block.scalar
            def _(act):
                def copy_out(g, b):
                    e = g * QUAD + b
                    act.wait_ge(d["y_done"], e + 1)
                    if not (is_first(g) and b < 2):
                        if b >= 0:
                            act.wait_ge(stored[b % 2], g * 32 + b // 2 * 16)
                        else:
                            act.wait_ge(stored[1], g * 32 - 16)
                    act.activation(out[:, b % 2], y_ps[:, :, :], ACT.Copy).then_inc(d["y_copied"], 1)

                def quad(g):
                    for b in range(QUAD):
                        e = g * QUAD + b
                        act.wait_ge(d["up_done"], e + 1)
                        if not (is_first(g) and b < 2):
                            act.wait_ge(d["hid_done"], e - 1)
                        expert_gate(act, up(b % 2), gate[:, b % 2], d["gate_done"])
                        if not (is_first(g) and b == 0):
                            copy_out(g, b - 1)

                rounds(act, quad)
                copy_out(NG4, -1)

            @block.vector
            def _(dve):
                def copy_in(g, b):
                    e = g * QUAD + b
                    dve.wait_ge(d["x_turned"], e + 1)
                    if not (is_first(g) and b < 2):
                        dve.wait_ge(d["up_done"], e - 1)
                    dve.tensor_copy(xT[:, b % 2], x_ps[:, :, :]).then_inc(d["x_copied"], 1)

                def quad(g):
                    for b in range(QUAD):
                        e = g * QUAD + b
                        if not (is_last(g) and b == QUAD - 1):
                            copy_in(g, b + 1)
                        dve.wait_ge(d["gate_done"], e * 2 + 2)
                        if not (is_first(g) and b < 2):
                            dve.wait_ge(d["y_done"], e - 1)
                        expert_hidden(dve, up(b % 2), gate[:, b % 2], hid[:, b % 2]).then_inc(d["hid_done"], 1)

                for b in range(bufs):
                    i = dve.memset(wgv[:, b, :, FE:VC], 0.0)
                i.then_inc(d["padded"], 1)
                copy_in(0, 0)
                rounds(dve, quad)


def moe_overflow(nc, m, c, a, slots, wgv, wo, over_table):
    FREE_Y = QUAD + 1
    with ExitStack() as ctx:
        l = Mem(nc, ctx)
        rows = l.sb("orows", [P, 2 * QUAD, D])
        xT = l.sb("orowsT", [P, QUAD, DK, P])
        gate = l.sb("ov_gate", [P, QUAD, 2, P])
        hid = l.sb("ov_hid", [P, QUAD, 2, P])
        out = l.sb("ov_out", [P, QUAD, D])
        up_ps = l.ps("ov_up_ps", [P, QUAD, 512])
        x_ps = l.ps("ov_x_ps", [P, QUAD, DK, P])
        y_ps = l.ps("ov_y_ps", [P, QUAD, D])
        loaded = [m.sem(f"ov_loaded{b}") for b in range(2 * QUAD)]
        d = sems(m, "ov", "x_turned x_copied up_done gate_done hid_done y_done y_copied stored out_free")
        region = slots[OVER0:ROWS, :].rearrange("(e p) d -> e p d", p=P)
        ROUND = LOADS + 16

        def up(b):
            return [up_ps[:, b, j * P:(j + 1) * P] for j in range(3)]

        def rounds(eng, quad):
            tiles = eng.value_load(over_table[0:1, NOVER:NOVER + 1], min_val=0, max_val=NOVER)
            with eng.Fori(0, NOVER // QUAD // 2) as pair:
                for q in range(2):
                    n = pair * 2 + q
                    with eng.If(n * QUAD < tiles):
                        quad(pair, n, q)

        with nc.Block() as block:

            @block.sync
            def _(sp):
                def quad(pair, n, q):
                    for b in range(QUAD):
                        u = q * QUAD + b
                        i = n * QUAD + b
                        if b == 0:
                            sp.wait_ge(d["y_done"], n * QUAD + (FREE_Y - QUAD))
                        own = sp.value_load(over_table[0:1, bass.ds(i, 1)], min_val=0, max_val=NE - 1)
                        sp.dma_start(rows[:, u, :], region[bass.ds(i, 1)].rearrange("o p d -> (o p) d")
                                     ).then_inc(loaded[u], 16)
                        load_expert(sp, wgv[:, u], wo[:, u], loaded[u],
                                    *(a[f"L0_ffn_w{s}"][bass.ds(own, 1)].rearrange("o r n -> (o r) n") for s in "gvo"))

                rounds(sp, quad)

            @block.tensor
            def _(pe):
                def quad(pair, n, q):
                    for b in range(QUAD):
                        u = q * QUAD + b
                        pe.wait_ge(loaded[u], pair * ROUND + ROUND)
                        if b % 2 == 0:
                            pe.wait_ge(d["x_copied"], n * 2 + (b // 2 + 1))
                        for k in range(DK):
                            i = pe.transpose(x_ps[:, b, k, :], rows[:, u, k * P:(k + 1) * P], c.ident[:, :])
                        i.then_inc(d["x_turned"], 1)
                    for b in range(QUAD):
                        u = q * QUAD + b
                        if b % 2 == 0:
                            pe.wait_ge(d["x_copied"], n * 2 + (b // 2 + 3))
                        pe.wait_ge(d["hid_done"], n * QUAD + (b + 1))
                        expert_up(pe, wgv[:, u], xT[:, b], up(b)).then_inc(d["up_done"], 1)
                    for b in range(QUAD):
                        u = q * QUAD + b
                        pe.wait_ge(d["hid_done"], n * QUAD + (b + 1 + QUAD))
                        if b % 2 == 0:
                            pe.wait_ge(d["y_copied"], n * 2 + (b // 2 + 1))
                        expert_down(pe, hid[:, b], wo[:, u], y_ps[:, b, :], 0).then_inc(d["y_done"], 1)

                pe.sem_inc(d["y_done"], FREE_Y)
                pe.sem_inc(d["up_done"], QUAD)
                rounds(pe, quad)

            @block.scalar
            def _(act):
                def quad(pair, n, q):
                    for b in range(QUAD):
                        act.wait_ge(d["up_done"], n * QUAD + (b + 1 + QUAD))
                        act.wait_ge(d["hid_done"], n * QUAD + (b + 1))
                        expert_gate(act, up(b), gate[:, b], d["gate_done"])
                    for h in range(2):
                        act.wait_ge(d["y_done"], n * QUAD + (2 * h + 2 + FREE_Y))
                        act.wait_ge(d["out_free"], n * 2 + (h + 1))
                        act.activation(out[:, 2 * h:2 * h + 2, :], y_ps[:, 2 * h:2 * h + 2, :], ACT.Copy
                                       ).then_inc(d["y_copied"], 1)

                act.sem_inc(d["y_copied"], 2)
                rounds(act, quad)

            @block.vector
            def _(dve):
                def quad(pair, n, q):
                    for h in range(2):
                        dve.wait_ge(d["x_turned"], n * QUAD + (2 * h + 2))
                        dve.wait_ge(d["up_done"], n * QUAD + (2 * h + 2))
                        dve.tensor_copy(xT[:, 2 * h:2 * h + 2], x_ps[:, 2 * h:2 * h + 2]).then_inc(d["x_copied"], 1)
                    for b in range(QUAD):
                        dve.wait_ge(d["gate_done"], n * (2 * QUAD) + (2 * b + 2))
                        dve.wait_ge(d["y_done"], n * QUAD + (b + 1 + FREE_Y - QUAD))
                        expert_hidden(dve, up(b), gate[:, b], hid[:, b]).then_inc(d["hid_done"], 1)

                dve.sem_inc(d["x_copied"], 2)
                dve.sem_inc(d["hid_done"], QUAD)
                rounds(dve, quad)

            @block.gpsimd
            def _(pool):
                def quad(pair, n, q):
                    for h in range(2):
                        pool.wait_ge(d["y_copied"], n * 2 + (h + 3))
                        pool.dma_start(region[bass.ds(n * QUAD + 2 * h, 2)].rearrange("o p d -> p o d"),
                                       out[:, 2 * h:2 * h + 2, :]).then_inc(d["stored"], 16)
                    pool.wait_ge(d["stored"], n * 32 + 32)
                    pool.sem_inc(d["out_free"], 2)

                pool.sem_inc(d["out_free"], 2)
                rounds(pool, quad)


def moe_combine(nc, m, x, slot, weight, slots):
    RING = 6
    with ExitStack() as ctx:
        l = Mem(nc, ctx)
        got = l.sb("got", [P, RING, TOPK, D])
        gathered = [m.sem(f"gathered{r}") for r in range(RING)]
        added = m.sem("cb_added")
        with nc.Block() as block:

            @block.gpsimd
            def _(pool):
                for t in range(TB):
                    if t >= RING:
                        pool.wait_ge(added, (t - RING + 1) * TOPK)
                    for j in range(TOPK):
                        pool.indirect_dma_start(got[:, t % RING, j, :], None, slots,
                                                bass.IndirectOffsetOnAxis(ap=slot[:, t, j:j + 1], axis=0)
                                                ).then_inc(gathered[t % RING], 16)

            @block.vector
            def _(dve):
                for t in range(TB):
                    dve.wait_ge(gathered[t % RING], (t // RING + 1) * TOPK * 16)
                    for j in range(TOPK):
                        if j:
                            dve.wait_ge(added, t * TOPK + j)
                        dve.scalar_tensor_tensor(x[:, t, :], got[:, t % RING, j, :], weight[:, t, j:j + 1], x[:, t, :],
                                                 ALU.mult, ALU.add).then_inc(added, 1)


def layer0_moe(nc, m, c, a, work, x, slot, weight, slots, cleared, prepare):
    with ExitStack() as ctx:
        l = Mem(nc, ctx)
        over_table = l.sb("over_table", [1, NOVER + 1], mybir.dt.int32)
        with ExitStack() as ctx2:
            l2 = Mem(nc, ctx2)
            xT = l2.sb("xT_moe", [P, DK, T * P])
            with ExitStack() as ctx3:
                l3 = Mem(nc, ctx3)
                mean_var = l3.sb("mean_var2", [P, T, 2])
                rstd = l3.sb("rstd2", [P, T])
                layernorm_stats(nc, m, "ln2", x, mean_var, rstd)
                normalise_all(nc, m, "ln2", x, mean_var, rstd, work)
            moe_route(nc, m, c, a, work, xT, slot, weight, over_table)
            moe_scatter(nc, m, c, a, x, work, xT, slot, slots, cleared, prepare)
        with ExitStack() as ctx2:
            l2 = Mem(nc, ctx2)
            wgv = l2.sb("ex_wgv", [P, 2 * QUAD, DK, WC])
            wo = l2.sb("ex_wo", [P, 2 * QUAD, 2, D])
            moe_experts(nc, m, c, a, slots, wgv, wo, 2 * QUAD)
            moe_overflow(nc, m, c, a, slots, wgv, wo, over_table)
        moe_combine(nc, m, x, slot, weight, slots)


H1, DN, DR, DV, R, QLR = 16, 128, 64, 128, 64, 192
QC = QLR // 2
KV = R + DR
RMS_EPS = 1e-6
SM1 = float(DN + DR) ** -0.5
HP = H1 // 2


def l1_weights(block, nc, m, c, a, w_a, w_q, w_o, kv_gain, rope):
    with ExitStack() as ctx:
        l = Mem(nc, ctx)
        q_b = l.sb("q_b", [QC, 2, H1, DN + DR])
        kv_b = l.sb("kv_b", [R, H1, DN + DV])
        o_raw = l.sb("o_raw", [P, H1, D])
        q_gain = l.sb("q_gain", [QC, 2])
        turned = l.sb("w1_turned", [P, 2, 2 * QC + 2 * R])
        turn_ps = l.ps("w1_turn_ps", [P, 2, 512])
        abs_ps = l.ps("w1_abs_ps", [P, 2, 512])
        out_ps = l.ps("w1_out_ps", [P, 2, 512])
        d = sems(m, "w1", "loaded turn_done copied abs_done abs_read out_done out_read")

        @block.sync
        def _(sp):
            sp.dma_start(q_b[:, :, :, :], a["L1_attn_w_q_b"].rearrange("(k p) (h n) -> p k h n", p=QC, h=H1)
                         ).then_inc(d["loaded"], 16)
            sp.dma_start(kv_b[:, :, :], a["L1_attn_w_kv_b"].rearrange("p (h n) -> p h n", h=H1)
                         ).then_inc(d["loaded"], 16)
            sp.dma_start(o_raw[:, :, :], a["L1_attn_w_o"].rearrange("(h p) n -> p h n", p=P)
                         ).then_inc(d["loaded"], 16)
            sp.dma_start(w_a[:, :, 0:QLR], a["L1_attn_w_q_a"].rearrange("(k p) n -> p k n", p=P)
                         ).then_inc(d["loaded"], 16)
            sp.dma_start(w_a[:, :, QLR:QLR + KV], a["L1_attn_w_kv_a"].rearrange("(k p) n -> p k n", p=P)
                         ).then_inc(d["loaded"], 16)
            sp.dma_start(rope[:, :, :, :], a["rope_table"]).then_inc(d["loaded"], 16)
            sp.dma_start(kv_gain[:, :], a["L1_attn_kv_a_ln_w"][None, :].partition_broadcast(P)
                         ).then_inc(d["loaded"], 16)
            with nc.allow_non_contiguous_dma(reason="a vector of 192 onto partitions"):
                sp.dma_start(q_gain[:, :], a["L1_attn_q_a_ln_w"].rearrange("(k p) -> p k", p=QC)
                             ).then_inc(d["loaded"], 16)

        @block.tensor
        def _(pe):
            def turn(h):
                u = h % 2
                reuse(pe, d["copied"], h, 2)
                for k in range(2):
                    pe.transpose(turn_ps[:, u, k * QC:(k + 1) * QC], q_b[:, k, h, 0:DN], c.ident[0:QC, 0:QC])
                pe.transpose(turn_ps[:, u, QLR:QLR + R], kv_b[:, h, 0:DN], c.ident[0:R, 0:R])
                pe.transpose(turn_ps[:, u, QLR + R:QLR + 2 * R], kv_b[:, h, DN:DN + DV], c.ident[0:R, 0:R]
                             ).then_inc(d["turn_done"], 1)

            pe.wait_ge(d["loaded"], 16 * 8)
            turn(0)
            for h in range(H1):
                u = h % 2
                if h + 1 < H1:
                    turn(h + 1)
                pe.wait_ge(d["copied"], h + 1)
                reuse(pe, d["abs_read"], h, 2)
                for k in range(2):
                    i = pe.matmul(abs_ps[0:QC, u, k * R:(k + 1) * R], turned[:, u, k * QC:(k + 1) * QC],
                                  turned[:, u, QLR:QLR + R], start=True, stop=True)
                i.then_inc(d["abs_done"], 1)
                reuse(pe, d["out_read"], h, 2)
                pe.matmul(out_ps[R * u:R * u + R, u, 0:D], turned[:, u, QLR + R:QLR + 2 * R], o_raw[:, h, :],
                          start=True, stop=True).then_inc(d["out_done"], 1)

        @block.scalar
        def _(act):
            for h in range(H1):
                act.wait_ge(d["turn_done"], h + 1)
                reuse(act, d["out_done"], h, 2)
                act.activation(turned[:, h % 2, :], turn_ps[:, h % 2, 0:QLR + 2 * R], ACT.Copy
                               ).then_inc(d["copied"], 1)

        @block.vector
        def _(dve):
            dve.wait_ge(d["loaded"], 16 * 8)
            for k in range(2):
                dve.tensor_scalar(w_q[:, k, :, R:KV], q_b[:, k, :, DN:DN + DR], q_gain[:, k:k + 1], None, ALU.mult)
            for h in range(H1):
                u = h % 2
                dve.wait_ge(d["abs_done"], h + 1)
                for k in range(2):
                    i = dve.tensor_scalar(w_q[:, k, h, 0:R], abs_ps[0:QC, u, k * R:(k + 1) * R],
                                          q_gain[:, k:k + 1], None, ALU.mult)
                i.then_inc(d["abs_read"], 1)
                dve.wait_ge(d["out_done"], h + 1)
                dve.tensor_copy(w_o[R * u:R * u + R, h // 2, :], out_ps[R * u:R * u + R, u, 0:D]
                                ).then_inc(d["out_read"], 1)


def l1_project(nc, m, c, d, b, x, mean_var, rstd, w_a, w_q, kv_gain, rope, qT, kT, lat_head, lat_rest, late=None):
    n0 = TB * b
    if late is not None:
        slot, weight, slots, got = late
        RING = got.shape[1]
    FREE_T, FREE_Q = 2, 4
    with ExitStack() as ctx:
        l = Mem(nc, ctx, f"_{b}")
        xh = l.sb("xh1", [P, D])
        xhT = l.sb("xhT1", [P, DK, P])
        squares = l.sb("a_squares", [P, QLR])
        ms = l.sb("a_ms", [P, 2])
        std = l.sb("a_std", [P, 2])
        inv = l.sb("a_inv", [P, 2])
        qa = l.sb("qa", [P, QLR])
        kf = l.sb("kf", [P, KV])
        kro = l.sb("k_rot", [P, 2, DR])
        qaT = l.sb("qaT", [QC, 2, P])
        q_own = l.sb("q_own", [P, 2, 4, DR])
        q_oth = l.sb("q_oth", [P, 2, 4, DR])
        q = l.sb("q_tok", [P, H1, KV])
        ones = q[:, :, :].rearrange("p (t w h) n -> p t w h n", t=TB, w=2)[:, :, :, 0, 0:R]
        x_ps = l.ps("x1_ps", [P, 512])
        a_ps = l.ps("a1_ps", [P, 512])
        at_ps = l.ps("at1_ps", [P, 512])
        q_ps = l.ps("q1_ps", [P, 2, 512])
        t_ps = l.ps("qt1_ps", [P, 2, 512])
        q_v = [q_ps[:, i, :].rearrange("p (h n) -> p h n", h=4) for i in range(2)]

        def before(eng, used, t, per=1):
            if not isinstance(t, int) or t + n0 > 0:
                eng.wait_ge(used, (t + n0) * per)

        with nc.Block() as block:

            @block.tensor
            def _(pe):
                def turn_x(t):
                    pe.wait_ge(d["xh_done"], t + (n0 + 1))
                    before(pe, d["xhT_done"], t)
                    for k in range(DK):
                        i = pe.transpose(x_ps[:, k * P:(k + 1) * P], xh[:, k * P:(k + 1) * P], c.ident[:, :])
                    i.then_inc(d["xT_done"], 1)

                def project_a(t):
                    pe.wait_ge(d["xhT_done"], t + (n0 + 1))
                    before(pe, d["sq_done"], t, 2)
                    before(pe, d["qa_done"], t)
                    before(pe, d["k_mul_done"], t, 4)
                    for k in range(DK):
                        i = pe.matmul(a_ps[:, 0:QLR + KV], xhT[:, k, :], w_a[:, k, :], start=k == 0, stop=k == DK - 1)
                    i.then_inc(d["a_done"], 1)

                def turn_a(t):
                    pe.wait_ge(d["qa_done"], t + (n0 + 1))
                    pe.wait_ge(d["kf_done"], (t + (n0 + 1)) * 2)
                    before(pe, d["at_copied"], t, 2)
                    for k in range(2):
                        pe.transpose(at_ps[0:QC, k * P:(k + 1) * P], qa[:, k * QC:(k + 1) * QC], c.ident[:, :])
                    pe.transpose(at_ps[:, 2 * P:3 * P], kf[:, :], c.ident[:, :]).then_inc(d["at_done"], 1)

                def project_q(t):
                    pe.wait_ge(d["at_copied"], (t + (n0 + 1)) * 2)
                    for i in range(4):
                        if not (isinstance(t, int) and t + n0 == 0 and i < 2):
                            pe.wait_ge(d["q_abs"], (t + n0) * 4 + (i - 1))
                            pe.wait_ge(d["q_mul"], (t + n0) * 12 + 3 * (i - 1))
                        for k in range(2):
                            x = pe.matmul(q_ps[:, i % 2, :], qaT[:, k, :],
                                          w_q[:, k, 4 * i:4 * i + 4, :].rearrange("p h n -> p (h n)"),
                                          start=k == 0, stop=k == 1)
                        x.then_inc(d["q_done"], 1)

                def turn_q(t):
                    for i in range(4):
                        pe.wait_ge(d["q_rot"], (t + n0) * 4 + (i + 1))
                        pe.wait_ge(d["q_abs"], (t + n0) * 4 + (i + 1))
                        pe.wait_ge(d["qT_done"], (t + n0) * 4 + (FREE_T + i - 1))
                        for j in range(4):
                            x = pe.transpose(t_ps[:, i % 2, j * P:(j + 1) * P], q[:, 4 * i + j, :], c.ident[:, :])
                        x.then_inc(d["turned"], 1)

                if b == 0:
                    pe.sem_inc(d["turned"], FREE_Q)
                turn_x(0)
                project_a(0)
                turn_x(1)
                turn_a(0)

                def step(t):
                    if not isinstance(t, int) or t + 1 < TB:
                        project_a(t + 1)
                    if not isinstance(t, int) or t > 0:
                        turn_q(t - 1)
                    if not isinstance(t, int) or t + 2 < TB:
                        turn_x(t + 2)
                    project_q(t)
                    if not isinstance(t, int) or t + 1 < TB:
                        turn_a(t + 1)

                step(0)
                with pe.Fori(1, TB - 2) as t:
                    step(t)
                step(TB - 2)
                step(TB - 1)
                turn_q(TB - 1)

            @block.vector
            def _(dve):
                def normalise(t):
                    before(dve, d["xT_done"], t)
                    dve.tensor_scalar(xh[:, :], x[:, t + n0, :], mean_var[:, t + n0, 0:1], rstd[:, bass.ds(t + n0, 1)],
                                      ALU.subtract, ALU.mult).then_inc(d["xh_done"], 1)

                def latents(t):
                    n = t + (n0 + 1)
                    dve.wait_ge(d["sq_done"], n * 2)
                    dve.tensor_scalar(ms[:, 0:1], ms[:, 0:1], 1.0 / QLR, RMS_EPS, ALU.mult, ALU.add
                                      ).then_inc(d["eps_done"], 1)
                    dve.tensor_scalar(ms[:, 1:2], ms[:, 1:2], 1.0 / R, RMS_EPS, ALU.mult, ALU.add
                                      ).then_inc(d["eps_done"], 1)
                    k_pe = a_ps[:, QLR + R:QLR + KV]
                    half = DR // 2
                    before(dve, d["at_done"], t)
                    dve.tensor_tensor(kro[:, 0, :], k_pe, rope[:, t, 0, :], ALU.mult).then_inc(d["k_mul_done"], 1)
                    dve.tensor_tensor(kro[:, 1, 0:half], k_pe[:, half:DR], rope[:, t, 1, 0:half], ALU.mult
                                      ).then_inc(d["k_mul_done"], 1)
                    dve.tensor_tensor(kro[:, 1, half:DR], k_pe[:, 0:half], rope[:, t, 1, half:DR], ALU.mult
                                      ).then_inc(d["k_mul_done"], 1)
                    dve.wait_ge(d["std_done"], n)
                    dve.reciprocal(inv[:, :], std[:, :]).then_inc(d["inv_done"], 1)
                    dve.wait_ge(d["k_mul_done"], n * 4 - 1)
                    dve.tensor_tensor(kf[:, R:KV], kro[:, 0, :], kro[:, 1, :], ALU.add).then_inc(d["kf_done"], 1)
                    dve.wait_ge(d["inv_done"], n)
                    dve.tensor_scalar(qa[:, :], a_ps[:, 0:QLR], inv[:, 0:1], None, ALU.mult).then_inc(d["qa_done"], 1)
                    before(dve, d["v_done"], t)
                    dve.tensor_scalar(kf[:, 0:R], a_ps[:, QLR:QLR + R], inv[:, 1:2], None, ALU.mult
                                      ).then_inc(d["k_mul_done"], 1)
                    dve.wait_ge(d["k_mul_done"], n * 4)
                    dve.tensor_tensor(kf[:, 0:R], kf[:, 0:R], kv_gain[:, :], ALU.mult).then_inc(d["kf_done"], 1)

                def rotate(t):
                    half = DR // 2
                    for i in range(4):
                        n = (t + n0) * 4 + (i + 1)
                        v = q_v[i % 2]
                        own, oth = q_own[:, i % 2], q_oth[:, i % 2]

                        def table(w, lo, hi):
                            return rope[:, t, w, lo:hi].rearrange("p (o e) -> p o e", o=1).to_broadcast([P, 4, hi - lo])

                        dve.wait_ge(d["q_abs"], n)
                        dve.tensor_tensor(own, v[:, :, R:KV], table(0, 0, DR), ALU.mult).then_inc(d["q_mul"], 1)
                        dve.tensor_tensor(oth[:, :, 0:half], v[:, :, R + half:KV], table(1, 0, half), ALU.mult
                                          ).then_inc(d["q_mul"], 1)
                        dve.tensor_tensor(oth[:, :, half:DR], v[:, :, R:R + half], table(1, half, DR), ALU.mult
                                          ).then_inc(d["q_mul"], 1)
                        dve.wait_ge(d["q_mul"], n * 3)
                        dve.wait_ge(d["turned"], n)
                        dve.tensor_tensor(q[:, 4 * i:4 * i + 4, R:KV], own, oth, ALU.add).then_inc(d["q_rot"], 1)

                if b == 0:
                    dve.memset(ones[:, :, 0, :], 1.0).then_inc(d["one_done"], 1)
                    dve.memset(ones[:, :, 1, :], 0.0).then_inc(d["one_done"], 1)
                    dve.wait_ge(d["one_done"], 2)
                    dve.tensor_copy(lat_head[:, :, R:2 * R], ones[:, :, 0, :]).then_inc(d["ones_done"], 1)
                    dve.tensor_copy(lat_rest[:, :, R:2 * R], ones[:, :, 1, :]).then_inc(d["ones_done"], 1)
                normalise(0)
                latents(0)
                normalise(1)

                def add_late(t):
                    dve.wait_ge(d["late_got"], (t + 1) * TOPK * 16)
                    for j in range(TOPK):
                        if j:
                            dve.wait_ge(d["late_added"], t * TOPK + j)
                        dve.scalar_tensor_tensor(x[:, TB + t, :], got[:, t % RING, j, :], weight[:, TB + t, j:j + 1],
                                                 x[:, TB + t, :], ALU.mult, ALU.add).then_inc(d["late_added"], 1)

                def step(t):
                    if not isinstance(t, int) or t + 2 < TB:
                        normalise(t + 2)
                    if not isinstance(t, int) or t + 1 < TB:
                        latents(t + 1)
                    if late is not None and t > 0:
                        add_late(t - 1)
                    rotate(t)

                if late is not None:
                    for t in range(TB):
                        step(t)
                    add_late(TB - 1)
                else:
                    with dve.Fori(0, TB - 2) as t:
                        step(t)
                    step(TB - 2)
                    step(TB - 1)

            @block.scalar
            def _(act):
                def turned_x(t):
                    act.wait_ge(d["xT_done"], t + (n0 + 1))
                    before(act, d["a_done"], t)
                    act.activation(xhT[:, :, :], x_ps[:, 0:D].rearrange("p (k n) -> p k n", k=DK), ACT.Copy
                                   ).then_inc(d["xhT_done"], 1)

                def squares_of(t):
                    n = t + (n0 + 1)
                    act.wait_ge(d["a_done"], n)
                    before(act, d["inv_done"], t)
                    before(act, d["std_done"], t)
                    act.activation(squares[:, :], a_ps[:, 0:QLR], ACT.Square, accum_out=ms[:, 0:1]
                                   ).then_inc(d["sq_done"], 1)
                    act.wait_ge(d["sq_done"], n * 2 - 1)
                    act.activation(squares[:, 0:R], a_ps[:, QLR:QLR + R], ACT.Square, accum_out=ms[:, 1:2]
                                   ).then_inc(d["sq_done"], 1)
                    act.wait_ge(d["eps_done"], n * 2)
                    act.activation(std[:, :], ms[:, :], ACT.Sqrt).then_inc(d["std_done"], 1)

                def turned_a(t):
                    n = t + (n0 + 1)
                    act.wait_ge(d["at_done"], n)
                    before(act, d["q_done"], t, 4)
                    act.activation(qaT[:, :, :], at_ps[0:QC, 0:2 * P].rearrange("p (k n) -> p k n", k=2), ACT.Copy
                                   ).then_inc(d["at_copied"], 1)
                    act.activation(kT[:, bass.ds(t * P, P)], at_ps[:, 2 * P:3 * P], ACT.Copy).then_inc(d["at_copied"], 1)

                def plain_q(t):
                    for i in range(4):
                        n = (t + n0) * 4 + (i + 1)
                        act.wait_ge(d["q_done"], n)
                        act.wait_ge(d["turned"], n)
                        act.activation(q[:, 4 * i:4 * i + 4, 0:R], q_v[i % 2][:, :, 0:R], ACT.Copy
                                       ).then_inc(d["q_abs"], 1)

                def turned_q(t):
                    for i in range(4):
                        act.wait_ge(d["turned"], (t + n0) * 4 + (i + 1 + FREE_Q))
                        act.activation(qT[:, 4 * i:4 * i + 4, bass.ds(t * P, P)],
                                       t_ps[:, i % 2, :].rearrange("p (h n) -> p h n", h=4), ACT.Copy
                                       ).then_inc(d["qT_done"], 1)

                if b == 0:
                    act.sem_inc(d["qT_done"], FREE_T)
                turned_x(0)
                squares_of(0)
                turned_x(1)
                turned_a(0)

                def step(t):
                    if not isinstance(t, int) or t + 1 < TB:
                        squares_of(t + 1)
                    if not isinstance(t, int) or t > 0:
                        turned_q(t - 1)
                    if not isinstance(t, int) or t + 2 < TB:
                        turned_x(t + 2)
                    plain_q(t)
                    if not isinstance(t, int) or t + 1 < TB:
                        turned_a(t + 1)

                step(0)
                with act.Fori(1, TB - 2) as t:
                    step(t)
                step(TB - 2)
                step(TB - 1)
                turned_q(TB - 1)

            @block.gpsimd
            def _(pool):
                pool.wait_ge(d["ones_done"], 2)
                for t in range(TB):
                    pool.wait_ge(d["kf_done"], (t + (n0 + 1)) * 2)
                    pool.tensor_copy(lat_head[:, t, 0:R], kf[:, 0:R]).then_inc(d["vh_done"], 1)
                    pool.wait_ge(d["vh_done"], t + (n0 + 1))
                    pool.tensor_tensor(lat_rest[:, t, 0:R], kf[:, 0:R], lat_head[:, t, 0:R], ALU.subtract
                                       ).then_inc(d["v_done"], 1)
                    if late is not None:
                        if t > 0:
                            pool.wait_ge(d["late_got"], t * TOPK * 16)
                        reuse(pool, d["late_added"], t, RING, TOPK)
                        for j in range(TOPK):
                            pool.indirect_dma_start(got[:, t % RING, j, :], None, slots, bass.IndirectOffsetOnAxis(
                                ap=slot[:, TB + t, j:j + 1], axis=0)).then_inc(d["late_got"], 16)


def l1_attend(nc, m, c, d, b, qT, kT, lat_head, lat_rest, oT, w, inv, shiftT):
    LAG = 2
    ROWS = [(qt, k0, min(512, (qt + 1) * P - k0)) for qt in range(TB) for k0 in range(0, (qt + 1) * P, 512)]
    NR = len(ROWS)
    COLS = [(qh, kt, max(0, kt - 4 * qh) * P) for qh in range(2) for kt in range(4 * qh + 4)]
    NC = len(COLS)
    LAST = [3, NC - 1]
    AHEAD = {0: (0, 1), 1: (2,), 2: (3,), 4: (4, 5), 5: (6, 7), 6: (8,), 7: (9,), 8: (10,), 9: (11,)}
    h0 = H1 * b
    FREE_S, FREE_W, FREE_O, FREE_M = 2, 3, 2, 2
    FREE_R = 3
    with ExitStack() as ctx:
        l = Mem(nc, ctx, f"_{b}")
        piece_max = l.sb("piece_max", [P, TB, 2])
        row_max = l.sb("row_max1", [P, TB])
        rest = l.sb("rest1", [P, TB])
        shift = l.sb("shift1", [P, TB, 3], BF16)
        w_head, w_rest = l.sb("w_head", [P, 3, 512], F32R), l.sb("w_rest", [P, 3, 512], F32R)
        k_head, k_rest = l.sb("k_head", [P, S], F32R), l.sb("k_rest", [P, S], F32R)
        q_head, q_rest = l.sb("q_head", [P, 2, 512], F32R), l.sb("q_rest", [P, 2, 512], F32R)
        s_ps = l.ps("s1_ps", [P, 2, 512])
        m_ps = l.ps("m1_ps", [P, 2, 512])
        o_ps = l.ps("o1_ps", [P, 2, 512])
        t_ps = l.ps("t1_ps", [P, TB, P], BF16)
        q_top = qT[:, :, :].bitcast(BF16).rearrange("p h (n e) -> p h n e", e=2)[:, :, :, 1]
        k_top = kT.bitcast(BF16).rearrange("p (n e) -> p n e", e=2)[:, :, 1]
        with nc.Block() as block:

            @block.tensor
            def _(pe):
                def row_scores(h, r):
                    qt, k0, n = ROWS[r]
                    diagonal = k0 + n == (qt + 1) * P
                    pe.wait_ge(d["max_done"], (h + h0) * NR + (FREE_M + r - 1))
                    i = pe.matmul(m_ps[:, r % 2, 0:n], q_top[:, h, qt * P:(qt + 1) * P], k_top[:, k0:k0 + n],
                                  start=True, stop=not diagonal)
                    if diagonal:
                        i = pe.matmul(m_ps[:, r % 2, n - P:n], c.identb[:, :], c.mask_qk[:, :], start=False, stop=True)
                    i.then_inc(d["m_done"], 1)

                def turn_shift(h):
                    pe.wait_ge(d["parts_done"], h + (h0 + 1))
                    if not (isinstance(h, int) and h + h0 == 0):
                        pe.wait_ge(d["sh_copied"], h + h0)
                    for qt in range(TB):
                        i = pe.transpose(t_ps[0:3, qt, :], shift[:, qt, :], c.identb[:, :])
                    i.then_inc(d["shT_done"], 1)

                def scores(h, u_h, s):
                    qh, kt, c0 = COLS[s]
                    u = s % 2
                    pe.wait_ge(d["w_done"], (h + h0) * NC + (FREE_S + s - 1))
                    q0 = qh * 512 + c0
                    if kt == 0:
                        pe.wait_ge(d["q_rest_done"], (h + h0) * 2 + (qh + 1))
                    keys = slice(kt * P, (kt + 1) * P)
                    for i, (ks, qs) in enumerate(((k_head, q_head), (k_head, q_rest), (k_rest, q_head))):
                        pe.matmul(s_ps[:, u, c0:512], ks[:, keys], qs[:, qh, c0:512], start=i == 0, stop=False)
                    diagonal = kt >= 4 * qh
                    if s == 0:
                        pe.wait_ge(d["sh_copied"], h + (h0 + 1))
                    i = pe.matmul(s_ps[:, u, c0:512], c.ones3[:, :], shiftT[:, u_h, q0:qh * 512 + 512],
                                  start=False, stop=not diagonal)
                    if diagonal:
                        i = pe.matmul(s_ps[:, u, c0:c0 + P], c.identb[:, :], c.mask_kq[:, :], start=False, stop=True)
                    i.then_inc(d["s_done"], 1)

                def outputs(h, s):
                    qh, kt, c0 = COLS[s]
                    pe.wait_ge(d["w_rest_done"], (h + h0) * NC + (FREE_R + s + 1))
                    if kt == 0:
                        pe.wait_ge(d["o_read"], (h + h0) * 2 + (FREE_O + qh - 1))
                    for i, (ls, ws) in enumerate(((lat_head, w_head), (lat_head, w_rest), (lat_rest, w_head))):
                        x = pe.matmul(o_ps[:, qh, c0:512], ls[:, kt, :], ws[:, s % 3, c0:512], start=kt == 0 and i == 0,
                                      stop=s in LAST and i == 2)
                    x.then_inc(d["pv_done"], 1)

                def head(h, u, ahead, behind=True):
                    for s in range(NC):
                        if s == 0:
                            pe.wait_ge(d["k_rest_done"], 2 * b + 2)
                        scores(h, u, s)
                        if ahead:
                            for r in AHEAD.get(s, ()):
                                row_scores(h + 1, r)
                        if s >= LAG:
                            outputs(h, s - LAG)
                        elif behind:
                            outputs(h - 1, s - LAG + NC)
                        if ahead and s == 11:
                            turn_shift(h + 1)

                if b == 0:
                    pe.sem_inc(d["pv_done"], FREE_W)
                for r in range(NR):
                    row_scores(0, r)
                turn_shift(0)
                head(0, 0, True, behind=False)
                head(1, 1, True)
                with pe.Fori(1, HP - 1) as pair:
                    head(pair * 2, 0, True)
                    head(pair * 2 + 1, 1, True)
                head(H1 - 2, 0, True)
                head(H1 - 1, 1, False)
                for s in range(NC - LAG, NC):
                    outputs(H1 - 1, s)

            @block.vector
            def _(dve):
                def maximum(h, r):
                    qt, k0, n = ROWS[r]
                    dve.wait_ge(d["m_done"], (h + h0) * NR + (r + 1))
                    dve.tensor_reduce(piece_max[:, qt, k0 // 512:k0 // 512 + 1], m_ps[:, r % 2, 0:n], AX.X, ALU.max
                                      ).then_inc(d["max_done"], 1)

                def parts(h):
                    n = h + h0
                    dve.wait_ge(d["max_done"], (h + h0) * NR + (FREE_M + NR))
                    dve.tensor_copy(row_max[:, 0:4], piece_max[:, 0:4, 0]).then_inc(d["comb_done"], 1)
                    dve.tensor_reduce(row_max[:, 4:8], piece_max[:, 4:8, :], AX.X, ALU.max).then_inc(d["comb_done"], 1)
                    dve.wait_ge(d["comb_done"], n * 2 + 2)
                    if not (isinstance(h, int) and n == 0):
                        dve.wait_ge(d["shT_done"], n)
                    dve.tensor_scalar(shift[:, :, 0], row_max[:, :], -1.0, None, ALU.mult).then_inc(d["neg_done"], 1)
                    dve.wait_ge(d["neg_done"], n + 1)
                    dve.scalar_tensor_tensor(rest[:, :], row_max[:, :], -1.0, shift[:, :, 0], ALU.mult, ALU.subtract
                                             ).then_inc(d["r_done"], 1)
                    dve.wait_ge(d["r_done"], n * 2 + 1)
                    dve.tensor_copy(shift[:, :, 1], rest[:, :]).then_inc(d["r_done"], 1)
                    dve.wait_ge(d["r_done"], n * 2 + 2)
                    dve.tensor_tensor(shift[:, :, 2], rest[:, :], shift[:, :, 1], ALU.subtract
                                      ).then_inc(d["parts_done"], 1)

                def invert(h, qh, j):
                    w_ = 512 // 4
                    dve.wait_ge(d["pv_done"], (h + h0) * NC + (FREE_W + LAST[qh] + 1))
                    dve.reciprocal(inv[R * qh:R * qh + R, j * w_:j * w_ + w_], o_ps[R:2 * R, qh, j * w_:j * w_ + w_]
                                   ).then_inc(d["inv2_done"], 1)

                def normalise(h, u, pair, qh):
                    dve.wait_ge(d["inv2_done"], (h + h0) * 8 + 4 * (qh + 1))
                    dve.tensor_tensor(oT[R * u:R * u + R, pair, qh * 512:qh * 512 + 512], o_ps[0:R, qh, :],
                                      inv[R * qh:R * qh + R, :], ALU.mult).then_inc(d["o_read"], 1)

                def query_rest(h, qh):
                    n = (h + h0) * 2 + (qh + 1)
                    dve.wait_ge(d["q_head_done"], n)
                    dve.tensor_tensor(q_rest[:, qh, :], qT[:, h, qh * 512:qh * 512 + 512], q_head[:, qh, :], ALU.subtract
                                      ).then_inc(d["q_rest_done"], 1)

                def head(h, u, pair, ahead, behind=True):
                    for r in range(NR):
                        if ahead:
                            maximum(h + 1, r)
                        if behind and r == 1:
                            query_rest(h, 1)
                        if behind and r in (2, 3, 4, 5):
                            invert(h - 1, 1, r - 2)
                        if behind and r == 6:
                            normalise(h - 1, 1 - u, pair if u else pair - 1, 1)
                        if r in (7, 8, 9, 10):
                            invert(h, 0, r - 7)
                    if ahead:
                        parts(h + 1)
                        query_rest(h + 1, 0)
                    normalise(h, u, pair, 0)

                if b == 0:
                    dve.sem_inc(d["max_done"], FREE_M)
                    dve.sem_inc(d["o_read"], FREE_O)
                for n in range(2):
                    dve.wait_ge(d["k_head_done"], 2 * b + n + 1)
                    half = slice(n * 512, (n + 1) * 512)
                    dve.tensor_tensor(k_rest[:, half], kT[:, half], k_head[:, half], ALU.subtract
                                      ).then_inc(d["k_rest_done"], 1)
                for r in range(NR):
                    maximum(0, r)
                parts(0)
                query_rest(0, 0)
                query_rest(0, 1)
                head(0, 0, 0, True, behind=False)
                head(1, 1, 0, True)
                with dve.Fori(1, HP - 1) as pair:
                    head(pair * 2, 0, pair, True)
                    head(pair * 2 + 1, 1, pair, True)
                head(H1 - 2, 0, HP - 1, True)
                head(H1 - 1, 1, HP - 1, False)
                for j in range(4):
                    invert(H1 - 1, 1, j)
                normalise(H1 - 1, 1, HP - 1, 1)

            @block.scalar
            def _(act):
                def weights(h, s):
                    qh, kt, c0 = COLS[s]
                    act.wait_ge(d["s_done"], (h + h0) * NC + (s + 1))
                    act.wait_ge(d["w_rest_done"], (h + h0) * NC + (FREE_R + s - 2))
                    act.activation(w[:, s % 3, c0:512], s_ps[:, s % 2, c0:512], ACT.Exp, scale=SM1
                                   ).then_inc(d["w_done"], 1)
                    act.wait_ge(d["w_done"], (h + h0) * NC + (FREE_S + s + 1))
                    act.wait_ge(d["pv_done"], (h + h0) * NC + (FREE_W + s - 2))
                    act.activation(w_head[:, s % 3, c0:512], w[:, s % 3, c0:512], ACT.Copy
                                   ).then_inc(d["w_head_done"], 1)

                def query_head(h, qh):
                    if not (isinstance(h, int) and h + h0 == 0):
                        act.wait_ge(d["s_done"], (h + h0) * NC + (LAST[qh] + 1 - NC))
                    act.activation(q_head[:, qh, :], qT[:, h, qh * 512:qh * 512 + 512], ACT.Copy
                                   ).then_inc(d["q_head_done"], 1)

                def place_shift(h, u):
                    act.wait_ge(d["shT_done"], h + (h0 + 1))
                    act.activation(shiftT[:, u, :], t_ps[0:3, :, :].rearrange("p q n -> p (q n)"), ACT.Copy
                                   ).then_inc(d["sh_copied"], 1)

                def head(h, u, ahead):
                    for s in range(NC):
                        weights(h, s)
                        if ahead and s == 6:
                            query_head(h + 1, 0)
                    if ahead:
                        place_shift(h + 1, 1 - u)
                        query_head(h + 1, 1)

                if b == 0:
                    act.sem_inc(d["w_done"], FREE_S)
                for n in range(2):
                    half = slice(n * 512, (n + 1) * 512)
                    act.activation(k_head[:, half], kT[:, half], ACT.Copy).then_inc(d["k_head_done"], 1)
                query_head(0, 0)
                query_head(0, 1)
                place_shift(0, 0)
                with act.Fori(0, HP - 1) as pair:
                    head(pair * 2, 0, True)
                    head(pair * 2 + 1, 1, True)
                head(H1 - 2, 0, True)
                head(H1 - 1, 1, False)

            @block.gpsimd
            def _(pool):
                def rest(h, s):
                    qh, kt, c0 = COLS[s]
                    pool.wait_ge(d["pv_done"], (h + h0) * NC + (FREE_W + s - 2))
                    pool.wait_ge(d["w_head_done"], (h + h0) * NC + (s + 1))
                    pool.tensor_tensor(w_rest[:, s % 3, c0:512], w[:, s % 3, c0:512], w_head[:, s % 3, c0:512],
                                       ALU.subtract).then_inc(d["w_rest_done"], 1)

                if b == 0:
                    pool.sem_inc(d["w_rest_done"], FREE_R)
                with pool.Fori(0, H1) as h:
                    for s in range(NC):
                        rest(h, s)


def l1_output(block, d, b, oT, w_o, x, y_ps):
    n0 = TB * b

    @block.tensor
    def _(pe):
        for t in range(TB):
            reuse(pe, d["y_added"], t + n0, 2)
            for p in range(HP):
                i = pe.matmul(y_ps[:, t % 2, 0:D], oT[:, p, t * P:(t + 1) * P], w_o[:, p, :], start=p == 0,
                              stop=p == HP - 1)
            i.then_inc(d["y_done"], 1)

    @block.vector
    def _(dve):
        for t in range(TB):
            dve.wait_ge(d["y_done"], t + n0 + 1)
            dve.tensor_tensor(x[:, t + n0, :], x[:, t + n0, :], y_ps[:, t % 2, 0:D], ALU.add
                              ).then_inc(d["y_added"], 1)


def l1_weight_buffers(m):
    return (m.sb("w_a", [P, DK, QLR + KV]), m.sb("w_q", [QC, 2, H1, KV]), m.sb("w_o1", [P, HP, D]),
            m.sb("kv_gain", [P, R]), m.sb("rope", [P, TB, 2, DR]))


def layer1_attention(nc, m, c, a, work, x, w_a, w_q, w_o, kv_gain, rope, oT, late=None):
    if late is not None:
        rows = oT[:, :, :].rearrange("p h n -> p (h n)")[:, 0:5 * TOPK * D].rearrange("p (r j n) -> p r j n", r=5,
                                                                                       j=TOPK)
        late = (*late, rows)
    scratch = work[:, :, :].rearrange("p t d -> p (t d)")
    w = scratch[:, 0:3 * 512].rearrange("p (n c) -> p n c", n=3)
    inv = scratch[:, 3 * 512:4 * 512]
    kT = scratch[:, 4 * 512:6 * 512]
    shiftT = scratch[0:3, 6 * 512:8 * 512].bitcast(BF16).rearrange("p (u n) -> p u n", u=2)
    with ExitStack() as ctx:
        l = Mem(nc, ctx)
        mean_var = l.sb("mean_var3", [P, T, 2])
        rstd = l.sb("rstd3", [P, T])
        lat_head, lat_rest = l.sb("lat_head", [P, TB, 2 * R], F32R), l.sb("lat_rest", [P, TB, 2 * R], F32R)
        layernorm_stats(nc, m, "ln3a", x, mean_var, rstd, t0=0, t1=TB)
        qT = l.sb("qT1", [P, H1, S])
        d = sems(m, "l1", "xh_done xT_done xhT_done a_done sq_done eps_done std_done inv_done k_mul_done kf_done qa_done "
                 "at_done at_copied q_done q_abs q_mul q_rot turned qT_done v_done ones_done max_done m_done parts_done "
                 "shT_done sh_copied w_done s_done pv_done o_read comb_done neg_done r_done inv2_done y_done y_added one_done "
                 "late_got late_added vh_done k_head_done k_rest_done q_head_done q_rest_done w_head_done w_rest_done")
        for b in range(B):
            l1_project(nc, m, c, d, b, x, mean_var, rstd, w_a, w_q, kv_gain, rope, qT, kT, lat_head, lat_rest,
                       late if b == 0 else None)
            l1_attend(nc, m, c, d, b, qT, kT, lat_head, lat_rest, oT, w, inv, shiftT)
            if b < B - 1:
                with nc.psum_tensor("y1_ps_0", [P, 2, 512], F32) as y_ps, nc.Block() as block:
                    l1_output(block, d, b, oT, w_o, x, y_ps)
                layernorm_stats(nc, m, "ln3b", x, mean_var, rstd, t0=TB, t1=T)
    return d



F1 = 1024
FK = F1 // P


def ffn_weights(block, nc, m, c, a, w_up, w_down):
    with ExitStack() as ctx:
        l = Mem(nc, ctx)
        raw = l.sb("w13_raw", [P, 2, FK, D])
        raw2 = l.sb("w2_raw", [P, DK, F1])
        had = l.sb("hadamard", [P, P])
        w2T = l.sb("w2T", [P, FK, D])
        fly = l.sb("fly", [P, 2, FK, D])
        turn_ps = l.ps("wf_turn_ps", [P, 4, 512])
        had_ps = l.ps("wf_had_ps", [P, 2, 512])
        d = sems(m, "wf", "loaded turned copied had_done had_copied stage")

        @block.sync
        def _(sp):
            for i, n in enumerate(("W1", "W3")):
                sp.dma_start(raw[:, i, :, :], a[f"L1_ffn_{n}"].rearrange("(f p) n -> p f n", p=P)
                             ).then_inc(d["loaded"], 16)
            sp.dma_start(raw2[:, :, :], a["L1_ffn_W2"].rearrange("(k p) n -> p k n", p=P)).then_inc(d["loaded"], 16)
            sp.dma_start(had[:, :], a["hadamard_table"]).then_inc(d["loaded"], 16)

        @block.tensor
        def _(pe):
            pe.wait_ge(d["loaded"], 64)
            n = 0
            for f in range(FK):
                reuse(pe, d["copied"], n, 4)
                for k in range(DK):
                    i = pe.transpose(turn_ps[:, n % 4, k * P:(k + 1) * P], raw2[:, k, f * P:(f + 1) * P],
                                     c.ident[:, :])
                i.then_inc(d["turned"], 1)
                n += 1
            for w in range(2):
                for f in range(FK):
                    reuse(pe, d["copied"], n, 4)
                    for k in range(DK):
                        i = pe.transpose(turn_ps[:, n % 4, k * P:(k + 1) * P], raw[:, w, f, k * P:(k + 1) * P],
                                         c.ident[:, :])
                    i.then_inc(d["turned"], 1)
                    n += 1
            for f in range(FK):
                pe.wait_ge(d["copied"], f + 1)
                reuse(pe, d["had_copied"], f, 2)
                pe.matmul(had_ps[:, f % 2, 0:D], had[:, :], w2T[:, f, :], start=True, stop=True
                          ).then_inc(d["had_done"], 1)

        @block.scalar
        def _(act):
            n = 0
            for f in range(FK):
                act.wait_ge(d["turned"], n + 1)
                act.activation(w2T[:, f, :], turn_ps[:, n % 4, 0:D], ACT.Copy).then_inc(d["copied"], 1)
                n += 1
            for w in range(2):
                for f in range(FK):
                    act.wait_ge(d["turned"], n + 1)
                    act.activation(w_up[:, w, :, f * P:(f + 1) * P],
                                   turn_ps[:, n % 4, 0:D].rearrange("p (k n) -> p k n", k=DK), ACT.Copy
                                   ).then_inc(d["copied"], 1)
                    n += 1

        @block.vector
        def _(dve):
            for f in range(FK):
                dve.wait_ge(d["had_done"], f + 1)
                dve.tensor_copy(fly[:, 0, f, :], had_ps[:, f % 2, 0:D]).then_inc(d["had_copied"], 1)
            src = fly[:, 0]
            n = 0
            for i, step in enumerate((1, 2, 4)):
                dst = w_down[:, :, :] if step == 4 else fly[:, 1 - i % 2]
                s_, d_ = (y.rearrange("p (x e s) n -> p x e s n", e=2, s=step) for y in (src, dst))
                if i == 0:
                    dve.wait_ge(d["had_copied"], FK)
                else:
                    dve.wait_ge(d["stage"], n)
                for x in range(FK // (2 * step)):
                    for e, op in ((0, ALU.add), (1, ALU.subtract)):
                        dve.tensor_tensor(d_[:, x, e], s_[:, x, 0], s_[:, x, 1], op).then_inc(d["stage"], 1)
                        n += 1
                src = dst


def layer1_ffn(nc, m, c, a, x, w_up, w_down):
    CH = 512 // P
    NCH = T // CH
    with ExitStack() as ctx:
        l = Mem(nc, ctx)
        mean_var = l.sb("mean_var4", [P, T, 2])
        rstd = l.sb("rstd4", [P, T])
        layernorm_stats(nc, m, "ln4", x, mean_var, rstd)
        up_head = l.sb("up_head", [P, 2, DK, F1], F32R)
        down_head = l.sb("down_head", [P, FK, D], F32R)
        up_rest = l.sb("up_rest", [P, 2, DK, F1], F32R)
        down_rest = l.sb("down_rest", [P, FK, D], F32R)
        split_weights(nc, m, "ffn_split", [(w_up.rearrange("p w k n -> p (w k) n"),
                                            up_head[:, :, :, :].rearrange("p w k n -> p (w k) n"),
                                            up_rest[:, :, :, :].rearrange("p w k n -> p (w k) n")),
                                           (w_down[:, :, :], down_head[:, :, :], down_rest[:, :, :])])
        xh = l.sb("xh4", [P, CH, D])
        x_head = l.sb("x_head", [P, DK, CH * P], F32R)
        x_rest = l.sb("x_rest", [P, DK, CH * P], F32R)
        act_out = l.sb("silu_out", [P, 2, 512])
        hid = l.sb("hid", [P, 4, 512])
        hid_head = l.sb("hid_head", [P, FK, 512], F32R)
        hid_rest = l.sb("hid_rest", [P, FK, 512], F32R)
        x_ps = l.ps("x4_ps", [P, 2, 512])
        g_ps = l.ps("g4_ps", [P, 2, 512])
        u_ps = l.ps("u4_ps", [P, 2, 512])
        y_ps = l.ps("y4_ps", [P, 2, 512])
        d = sems(m, "ff", "xh_done x_turned x_copied x_rest_done hid_head_done hid_rest_done g_done u_done silu_done hid_done y_done y_added started")
        with nc.Block() as block:

            @block.tensor
            def _(pe):
                def turn(ch):
                    for k in range(DK):
                        for t in range(CH):
                            if k == 0:
                                pe.wait_ge(d["xh_done"], ch * CH + (t + 1))
                            if t == 0 and not (isinstance(ch, int) and ch == 0):
                                pe.wait_ge(d["x_rest_done"], ch * DK - (DK - 1 - k))
                            i = pe.transpose(x_ps[:, k, t * P:(t + 1) * P], xh[:, t, k * P:(k + 1) * P], c.ident[:, :])
                        i.then_inc(d["x_turned"], 1)

                def up(ch):
                    pe.wait_ge(d["x_rest_done"], ch * DK + DK)
                    for f in range(FK):
                        n = ch * FK + f
                        if not (isinstance(ch, int) and ch == 0 and f < 2):
                            pe.wait_ge(d["silu_done"], n - 1)
                        i = three_passes(pe, g_ps[:, f % 2, :], [
                            (up_head[:, 0, k, f * P:(f + 1) * P], up_rest[:, 0, k, f * P:(f + 1) * P],
                             x_head[:, k, :], x_rest[:, k, :]) for k in range(DK)])
                        i.then_inc(d["g_done"], 1)
                        if not (isinstance(ch, int) and ch == 0 and f < 2):
                            pe.wait_ge(d["hid_done"], n - 1)
                        i = three_passes(pe, u_ps[:, f % 2, :], [
                            (up_head[:, 1, k, f * P:(f + 1) * P], up_rest[:, 1, k, f * P:(f + 1) * P],
                             x_head[:, k, :], x_rest[:, k, :]) for k in range(DK)])
                        i.then_inc(d["u_done"], 1)

                def down(ch):
                    pe.wait_ge(d["hid_rest_done"], ch * FK + FK)
                    for t in range(CH):
                        if not (isinstance(ch, int) and ch == 0 and t < 2):
                            pe.wait_ge(d["y_added"], ch * CH + (t - 1))
                        i = three_passes(pe, y_ps[:, t % 2, 0:D], [
                            (hid_head[:, f, t * P:(t + 1) * P], hid_rest[:, f, t * P:(t + 1) * P],
                             down_head[:, f, :], down_rest[:, f, :]) for f in range(FK)])
                        i.then_inc(d["y_done"], 1)

                turn(0)
                up(0)
                turn(1)
                down(0)
                with pe.Fori(1, NCH - 1) as ch:
                    up(ch)
                    turn(ch + 1)
                    down(ch)
                up(NCH - 1)
                down(NCH - 1)

            @block.scalar
            def _(act):
                def turned(ch):
                    for k in range(DK):
                        act.wait_ge(d["x_turned"], ch * DK + (k + 1))
                        act.activation(x_head[:, k, :], x_ps[:, k, :], ACT.Copy).then_inc(d["x_copied"], 1)

                def hidden_head(ch, f):
                    act.wait_ge(d["hid_done"], ch * FK + (f + 1))
                    if f == 0 and not (isinstance(ch, int) and ch == 0):
                        act.wait_ge(d["y_done"], ch * CH)
                    act.activation(hid_head[:, f, :], hid[:, f % 4, :], ACT.Copy).then_inc(d["hid_head_done"], 1)

                def gate(ch):
                    for f in range(FK):
                        if f > 1:
                            hidden_head(ch, f - 2)
                        n = ch * FK + f
                        act.wait_ge(d["g_done"], n + 1)
                        if not (isinstance(ch, int) and ch == 0 and f < 2):
                            act.wait_ge(d["hid_done"], n - 1)
                        act.activation(act_out[:, f % 2, :], g_ps[:, f % 2, :], ACT.Silu).then_inc(d["silu_done"], 1)
                    for f in (FK - 2, FK - 1):
                        hidden_head(ch, f)

                turned(0)
                gate(0)
                with act.Fori(1, NCH) as ch:
                    act.wait_ge(d["u_done"], ch * FK)
                    turned(ch)
                    gate(ch)

            @block.vector
            def _(dve):
                def normalise(ch):
                    for t in range(CH):
                        if t == 0 and not (isinstance(ch, int) and ch == 0):
                            dve.wait_ge(d["x_turned"], ch * DK)
                        i = ch * CH + t
                        dve.tensor_scalar(xh[:, t, :], x[:, i, :], mean_var[:, i, 0:1], rstd[:, bass.ds(i, 1)],
                                          ALU.subtract, ALU.mult).then_inc(d["xh_done"], 1)

                def rest(ch):
                    for k in range(DK):
                        dve.wait_ge(d["x_copied"], ch * DK + (k + 1))
                        dve.tensor_tensor(x_rest[:, k, :], x_ps[:, k, :], x_head[:, k, :], ALU.subtract
                                          ).then_inc(d["x_rest_done"], 1)

                def hidden_rest(ch, f):
                    dve.wait_ge(d["hid_head_done"], ch * FK + (f + 1))
                    dve.tensor_tensor(hid_rest[:, f, :], hid[:, f % 4, :], hid_head[:, f, :], ALU.subtract
                                      ).then_inc(d["hid_rest_done"], 1)

                def hidden(ch):
                    for f in range(FK):
                        n = ch * FK + f
                        if f > 1:
                            hidden_rest(ch, f - 2)
                        dve.wait_ge(d["silu_done"], n + 1)
                        dve.wait_ge(d["u_done"], n + 1)
                        if f == 0 and not (isinstance(ch, int) and ch == 0):
                            dve.wait_ge(d["y_done"], ch * CH)
                        if not (isinstance(ch, int) and ch == 0 and f < 4):
                            dve.wait_ge(d["hid_rest_done"], n - 3)
                        dve.tensor_tensor(hid[:, f % 4, :], act_out[:, f % 2, :], u_ps[:, f % 2, :], ALU.mult
                                          ).then_inc(d["hid_done"], 1)
                    for f in (FK - 2, FK - 1):
                        hidden_rest(ch, f)

                def add(ch):
                    for t in range(CH):
                        i = ch * CH + t
                        dve.wait_ge(d["y_done"], ch * CH + (t + 1))
                        dve.tensor_tensor(x[:, i, :], x[:, i, :], y_ps[:, t % 2, 0:D], ALU.add).then_inc(d["y_added"], 1)

                normalise(0)
                rest(0)
                normalise(1)
                hidden(0)
                rest(1)
                add(0)
                with dve.Fori(1, NCH - 1) as ch:
                    normalise(ch + 1)
                    hidden(ch)
                    rest(ch + 1)
                    add(ch)
                hidden(NCH - 1)
                add(NCH - 1)


def transformer(nc, a, out):
    with ExitStack() as ctx:
        m = Mem(nc, ctx)
        c = Consts(m)
        work = m.sb("work", [P, T, D])
        loaded = [m.sem(f"x_loaded{i}") for i in range(4)]
        x_dram = a["L0_attn_x"].rearrange("b (t p) d -> p (b t) d", p=P)
        with nc.Block() as block:

            @block.sync
            def _(sp):
                for i in range(4):
                    sp.dma_start(work[:, 4 * i:4 * i + 4, :], x_dram[:, 4 * i:4 * i + 4, :]
                                 ).then_inc(loaded[i], 16)
        zero = m.sb("zero", [P, 1, P])
        constants(nc, m, c, zero)
        slots = nc.dram_tensor("slots", [ROWS, D], F32, kind="Internal").ap()
        cleared = m.sem("cleared")
        layer = Mem(nc, ctx)
        x = layer0_attention(nc, layer, c, a, work, x_dram, loaded, slots, zero, cleared)
        layer.free_semaphores()
        l1_weight = l1_weight_buffers(m)
        next_layer = Mem(nc, ctx)
        slot, weight = m.sb("slot", [P, T, TOPK], U32), m.sb("weight", [P, T, TOPK])
        layer = Mem(nc, ctx)
        layer0_moe(nc, layer, c, a, work, x, slot, weight, slots, cleared,
                   lambda block: l1_weights(block, nc, next_layer, c, a, *l1_weight))
        layer.free_semaphores()
        w_down = m.sb("w_down", [P, FK, D])
        with ExitStack() as ctx2:
            oT = Mem(nc, ctx2).sb("oT", [P, HP, S])
            layer = Mem(nc, ctx)
            late = (slot, weight, slots)
            d = layer1_attention(nc, layer, c, a, work, x, *l1_weight, oT, late)
            w_up = work[:, :, :].rearrange("p t d -> p (t d)").rearrange("p (w k n) -> p w k n", w=2, k=DK)
            with nc.psum_tensor("y1_ps_1", [P, 2, 512], F32) as y_ps, nc.Block() as block:
                l1_output(block, d, B - 1, oT, l1_weight[2], x, y_ps)
                ffn_weights(block, nc, next_layer, c, a, w_up, w_down)
            layer.free_semaphores()
        layer = Mem(nc, ctx)
        layer1_ffn(nc, layer, c, a, x, w_up, w_down)
        layer.free_semaphores()
        stored = m.sem("stored")
        with nc.Block() as block:

            @block.sync
            def _(sp):
                sp.dma_start(out.rearrange("b (t p) d -> p (b t) d", p=P), x[:, :, :]).then_inc(stored, 16)
                sp.wait_ge(stored, 16)
                sp.wait_ge(cleared, 16 * 8)


_INS = [
    "L0_attn_x", "L0_attn_ln_q_g", "L0_attn_ln_q_b", "L0_attn_Wq",
    "L0_attn_bq", "L0_attn_ln_kv_g", "L0_attn_ln_kv_b", "L0_attn_Wkv",
    "L0_attn_bkv", "L0_attn_ln_h_g", "L0_attn_ln_h_b", "L0_attn_Wo",
    "L0_attn_bo", "L0_ffn_w_router", "L0_ffn_wg", "L0_ffn_wv",
    "L0_ffn_wo", "L0_ffn_swg", "L0_ffn_swv", "L0_ffn_swo",
    "L1_attn_w_q_a", "L1_attn_q_a_ln_w", "L1_attn_w_q_b", "L1_attn_w_kv_a",
    "L1_attn_kv_a_ln_w", "L1_attn_w_kv_b", "L1_attn_w_o", "L1_ffn_W1",
    "L1_ffn_W2", "L1_ffn_W3",
]
_OUTS = [((2, 1024, 256), "float32")]


def kernel(**inputs):
    import numpy as _np
    import concourse.bacc as _bacc
    from concourse import mybir as _mybir
    from concourse.bass_utils import run_bass_kernel_spmd as _run

    nc = _bacc.Bacc("TRN2", target_bir_lowering=False, num_devices=1)
    given = {name: _np.ascontiguousarray(inputs[name]) for name in _INS}
    given.update(tables())
    arrays, args = {}, {}
    for name, a in given.items():
        arrays[f"in_{name}_dram"] = a
        args[name] = nc.dram_tensor(f"in_{name}_dram", a.shape, _mybir.dt.from_np(a.dtype), kind="ExternalInput").ap()
    outs = [nc.dram_tensor(f"out_{i}_dram", shape, _mybir.dt.from_np(_np.dtype(dtype)), kind="ExternalOutput").ap()
            for i, (shape, dtype) in enumerate(_OUTS)]
    transformer(nc, args, outs[0])
    r = _run(nc, [arrays], core_ids=[0])
    return r.results[0]["out_0_dram"]
```
